# Optimizing a Trainium2 kernel written in Bass

```python
import numpy as np
import jax
import jax.numpy as jnp

def _softmax(x, axis=-1):
    return jax.nn.softmax(x, axis=axis)

def _gelu(x):
    return jax.nn.gelu(x, approximate=True)

def _silu(x):
    return jax.nn.silu(x)

def _sigmoid(x):
    return jax.nn.sigmoid(x)

def _layernorm(x, axis=-1, eps=1e-05):
    m = jnp.mean(x, axis=axis, keepdims=True)
    v = jnp.var(x, axis=axis, keepdims=True)
    return (x - m) / jnp.sqrt(v + eps)

def _scatter_add(tgt, idx, src, axis=0):
    return tgt.at[idx].add(src)

def _segment_sum(src, seg, n):
    return jax.ops.segment_sum(src, seg, n)
kernel_name = 'mk_conv_seq_d1_conv_nhwc256_r2_3cfb64'

def setup_inputs(seed: int=0):
    np.random.seed(seed)
    _w = jnp.asarray

    def _rec_inputs():
        import jax
        import jax.numpy as jnp
        _gk = jax.random.key(seed)
        x = -0.0003929 + 0.9999 * jax.random.normal(jax.random.fold_in(_gk, 1), (16, 32, 32, 128), jnp.float32)
        return x
    x = _rec_inputs()

    def _L0_conv_setup():
        import math
        import jax, jax.numpy as jnp
        import numpy as np
        B, H, W, C = (16, 32, 32, 128)
        _POS = [(-1, -1), (-1, 0), (-1, 1), (0, -1), (0, 0), (0, 1), (1, -1), (1, 0), (1, 1)]

        def _local_attn(hn, w_qkv, b_qkv):
            Bb, Hh, Ww, Cc = hn.shape
            qkv = jnp.einsum('bhwc,dc->bhwd', hn, w_qkv) + b_qkv
            q, k, v = jnp.split(qkv, 3, axis=-1)
            kp = jnp.pad(k, ((0, 0), (1, 1), (1, 1), (0, 0)))
            vp = jnp.pad(v, ((0, 0), (1, 1), (1, 1), (0, 0)))
            scale = 1.0 / math.sqrt(Cc)
            scores = jnp.stack([(q * kp[:, 1 + dy:1 + dy + Hh, 1 + dx:1 + dx + Ww, :]).sum(-1) for dy, dx in _POS], axis=-1) * scale
            w = jax.nn.softmax(scores, axis=-1)
            out = jnp.zeros_like(v)
            for i, (dy, dx) in enumerate(_POS):
                out = out + w[..., i:i + 1] * vp[:, 1 + dy:1 + dy + Hh, 1 + dx:1 + dx + Ww, :]
            return out
        key = jax.random.key(seed)
        ks = jax.random.split(key, 6)
        return {'h': jax.random.normal(ks[0], (B, H, W, C), jnp.float32), 'w_perc': jax.random.normal(ks[1], (3 * C, 1, 3, 3), jnp.float32) * 0.1, 'b_perc': jnp.zeros((3 * C,), jnp.float32), 'w_up1': jax.random.normal(ks[2], (2 * C, 3 * C, 1, 1), jnp.float32) * 0.02, 'b_up1': jnp.zeros((2 * C,), jnp.float32), 'w_up2': jax.random.normal(ks[3], (C, 2 * C, 1, 1), jnp.float32) * 0.02, 'b_up2': jnp.zeros((C,), jnp.float32), 'w_qkv': jax.random.normal(ks[4], (3 * C, C), jnp.float32) * 0.02, 'b_qkv': jnp.zeros((3 * C,), jnp.float32)}
    _L0_conv_all = _L0_conv_setup()
    _L0_conv_in = {k: v for k, v in _L0_conv_all.items() if k in ('w_perc', 'b_perc', 'w_up1', 'b_up1', 'w_up2', 'b_up2', 'w_qkv', 'b_qkv')}
    del _L0_conv_all
    return {'x': x, 'L0_conv_w_perc': _L0_conv_in['w_perc'], 'L0_conv_b_perc': _L0_conv_in['b_perc'], 'L0_conv_w_up1': _L0_conv_in['w_up1'], 'L0_conv_b_up1': _L0_conv_in['b_up1'], 'L0_conv_w_up2': _L0_conv_in['w_up2'], 'L0_conv_b_up2': _L0_conv_in['b_up2'], 'L0_conv_w_qkv': _L0_conv_in['w_qkv'], 'L0_conv_b_qkv': _L0_conv_in['b_qkv']}

def reference(x, L0_conv_w_perc, L0_conv_b_perc, L0_conv_w_up1, L0_conv_b_up1, L0_conv_w_up2, L0_conv_b_up2, L0_conv_w_qkv, L0_conv_b_qkv):
    import jax
    import jax.numpy as jnp

    def _L0_conv_ref(h, w_perc, b_perc, w_up1, b_up1, w_up2, b_up2, w_qkv, b_qkv):
        import math
        import jax, jax.numpy as jnp
        import numpy as np
        B, H, W, C = (16, 32, 32, 128)
        _POS = [(-1, -1), (-1, 0), (-1, 1), (0, -1), (0, 0), (0, 1), (1, -1), (1, 0), (1, 1)]

        def _local_attn(hn, w_qkv, b_qkv):
            Bb, Hh, Ww, Cc = hn.shape
            qkv = jnp.einsum('bhwc,dc->bhwd', hn, w_qkv) + b_qkv
            q, k, v = jnp.split(qkv, 3, axis=-1)
            kp = jnp.pad(k, ((0, 0), (1, 1), (1, 1), (0, 0)))
            vp = jnp.pad(v, ((0, 0), (1, 1), (1, 1), (0, 0)))
            scale = 1.0 / math.sqrt(Cc)
            scores = jnp.stack([(q * kp[:, 1 + dy:1 + dy + Hh, 1 + dx:1 + dx + Ww, :]).sum(-1) for dy, dx in _POS], axis=-1) * scale
            w = jax.nn.softmax(scores, axis=-1)
            out = jnp.zeros_like(v)
            for i, (dy, dx) in enumerate(_POS):
                out = out + w[..., i:i + 1] * vp[:, 1 + dy:1 + dy + Hh, 1 + dx:1 + dx + Ww, :]
            return out
        Cc = h.shape[-1]
        x = jnp.transpose(h, (0, 3, 1, 2))
        perceived = jax.lax.conv_general_dilated(x, w_perc, window_strides=(1, 1), padding='SAME', feature_group_count=Cc, dimension_numbers=('NCHW', 'OIHW', 'NCHW')) + b_perc[None, :, None, None]
        hid = jnp.einsum('bphw,dp->bdhw', perceived, w_up1[:, :, 0, 0]) + b_up1[None, :, None, None]
        hid = jax.nn.gelu(hid, approximate=False)
        dx = jnp.einsum('bdhw,cd->bchw', hid, w_up2[:, :, 0, 0]) + b_up2[None, :, None, None]
        x_new = x + dx
        h_new = jnp.transpose(x_new, (0, 2, 3, 1))
        h_attn = _local_attn(h_new, w_qkv, b_qkv)
        return h_new + h_attn

    def _gn(v, G=32, eps=1e-05):
        B_, H_, W_, C_ = v.shape
        g = v.reshape(B_, H_, W_, G, C_ // G)
        m = jnp.mean(g, axis=(1, 2, 4), keepdims=True)
        s = jnp.var(g, axis=(1, 2, 4), keepdims=True)
        return ((g - m) / jnp.sqrt(s + eps)).reshape(v.shape)

    def _ln_c(v, eps=1e-06):
        m = jnp.mean(v, axis=-1, keepdims=True)
        s = jnp.var(v, axis=-1, keepdims=True)
        return (v - m) / jnp.sqrt(s + eps)

    def _ln_t(v, eps=1e-05):
        m = jnp.mean(v, axis=-1, keepdims=True)
        s = jnp.var(v, axis=-1, keepdims=True)
        return (v - m) / jnp.sqrt(s + eps)

    def _to_tokens(v):
        B_, H_, W_, C_ = v.shape
        return v.reshape(B_, H_ * W_, C_)

    def _from_tokens(t, like):
        return t.reshape(like.shape)
    x = _L0_conv_ref(x, L0_conv_w_perc, L0_conv_b_perc, L0_conv_w_up1, L0_conv_b_up1, L0_conv_w_up2, L0_conv_b_up2, L0_conv_w_qkv, L0_conv_b_qkv)
    return x

_drawn_inputs = setup_inputs


def setup_inputs(seed=0):
    import zlib

    import numpy as np

    out = dict(_drawn_inputs(seed))
    spreads = {'L0_conv_b_perc': (0.0, 0.8),
     'L0_conv_b_up1': (0.0, 0.524),
     'L0_conv_b_up2': (0.0, 0.1),
     'L0_conv_b_qkv': (0.0, 0.1)}
    factors = {'L0_conv_w_perc': 3.011, 'L0_conv_w_up1': 2.804}
    for name, (base, spread) in spreads.items():
        noise = np.random.default_rng([zlib.crc32(name.encode()), seed]).standard_normal(out[name].shape)
        drawn = base * np.exp(spread * noise) if base else spread * noise
        out[name] = jnp.asarray(drawn.astype(out[name].dtype))
    for name, factor in factors.items():
        out[name] = (out[name] * factor).astype(out[name].dtype)
    return out
```

```python
from contextlib import ExitStack

import numpy as np

import concourse.bass as bass
from concourse import mybir
from concourse.alu_op_type import AluOpType as ALU

ACT = mybir.ActivationFunctionType
AX = mybir.AxisListType
F32 = mybir.dt.float32
F32R = mybir.dt.float32r
BF16 = mybir.dt.bfloat16

P = 128
B, H, W, C = 16, 32, 32, 128
PIX = H * W
TR = P // W
T = H // TR
CH = 512
NCH = PIX // CH
CR = CH // W
HID = 2 * C
TAPS = [(dy, dx) for dy in range(3) for dx in range(3)]
HALO = 2 * W
NPAD = 6
SC = P + HALO + NPAD
NEG = -1e30
SCALE = float(C) ** -0.5


def window_masks():
    m = np.full((P, 4, SC), NEG, np.float32)
    for kind in range(4):
        for q in range(P):
            qy, qx = divmod(q, W)
            inside = 0
            for ky in range(-1, TR + 1):
                if abs(ky - qy) > 1 or (kind == 0 and ky < 0) or (kind == 3 and ky >= TR):
                    continue
                for kx in range(max(0, qx - 1), min(W, qx + 2)):
                    col = P + kx if ky < 0 else P + W + kx if ky >= TR else ky * W + kx
                    m[q, kind, col] = 0.0
                    inside += 1
            m[q, kind, P + HALO:P + HALO + 9 - inside] = 0.0
    return m


def build(nc, x, w_perc, b_perc, w_up1, b_up1, w_up2, b_up2, w_qkv, b_qkv, ident_c, mask_c, out):
    with ExitStack() as ctx:
        def sb(name, shape, dt=F32):
            return ctx.enter_context(nc.sbuf_tensor(name, shape, dt))

        def sem(name):
            return ctx.enter_context(nc.semaphore(name))

        bank = [ctx.enter_context(nc.psum_tensor(f"bank{i}", [P, CH], F32)) for i in range(8)]

        ident = sb("ident", [P, P])
        ident_bf = sb("ident_bf", [P, P], BF16)
        mask_f = sb("mask_f", [P, 4, SC])
        mask_bf = sb("mask_bf", [P, 4, SC], BF16)
        w1 = sb("w1", [P, 2, 3 * C])
        w2 = sb("w2", [P, HID])
        wqkv = sb("wqkv", [P, 3, C])
        wp = sb("wp", [P, 3, 9])
        bp = sb("bp", [P, 3])
        b1 = sb("b1", [P, 2])
        b2 = sb("b2", [P, 1])
        bqk = sb("bqk", [P, 2])
        bv = sb("bv", [P, C])
        w1T = sb("w1T", [P, 3, HID])
        w2T = sb("w2T", [P, 2, C])
        wqkvT = sb("wqkvT", [P, 3, C])
        b1eff = sb("b1eff", [P, 2])
        bq_s = sb("bq_s", [P, 1])
        weff = sb("weff", [P, 9, HID])
        whi = sb("whi", [P, 9, HID], F32R)
        wlo = sb("wlo", [P, 9, HID], F32R)

        x_in = sb("x_in", [P, 2, T, C])
        xhi = sb("xhi", [P, 2, H + 2, W + 2], F32R)
        xlo = sb("xlo", [P, 2, H + 2, W + 2], F32R)
        hid = sb("hid", [P, 2, PIX])
        h = sb("h", [P, PIX])
        q_sb = sb("q_sb", [P, PIX])
        k_sb = sb("k_sb", [P, PIX])
        v_sb = sb("v_sb", [P, T, C])
        v_halo = sb("v_halo", [HALO, T, C])
        negmax = sb("negmax", [P, T])
        psum_p = sb("psum_p", [P, T])
        rsum = sb("rsum", [P, T])
        p_sb = sb("p_sb", [P, T, SC])
        pt_main = sb("pt_main", [P, T, P])
        pt_halo = sb("pt_halo", [HALO, T, P])
        o_sb = sb("o_sb", [P, T, C])
        out_sb = sb("out_sb", [P, T, C])

        weights_in = sem("weights_in")
        x_loaded = [sem(f"x_loaded{i}") for i in range(2)]
        vh_done = sem("vh_done")
        stored = [sem(f"stored{i}") for i in range(2)]
        zeroed = sem("zeroed")
        wt_ready = sem("wt_ready")
        wt_copied = sem("wt_copied")
        b1_ready = sem("b1_ready")
        setup_dve = sem("setup_dve")
        whi_done = sem("whi_done")
        wlo_done = sem("wlo_done")
        consts_done = sem("consts_done")
        xt_ready = sem("xt_ready")
        conv_ready = sem("conv_ready")
        up_ready = sem("up_ready")
        q_ready = sem("q_ready")
        k_ready = sem("k_ready")
        v_ready = sem("v_ready")
        s_ready = sem("s_ready")
        pt_ready = sem("pt_ready")
        hp_ready = sem("hp_ready")
        o_ready = sem("o_ready")
        xhi_done = sem("xhi_done")
        hid_done = sem("hid_done")
        q_done = sem("q_done")
        p_done = sem("p_done")
        ptm_done = sem("ptm_done")
        xlo_done = sem("xlo_done")
        hx_done = sem("hx_done")
        h_done = sem("h_done")
        k_done = sem("k_done")
        v_done = sem("v_done")
        max_done = sem("max_done")
        pth_done = sem("pth_done")
        rsum_done = sem("rsum_done")
        om_done = sem("om_done")
        out_done = sem("out_done")

        x_dram = x.rearrange("b (t r) w c -> b (r w) t c", r=TR)
        out_dram = out.rearrange("b (t r) w c -> b (r w) t c", r=TR)
        N_W = 11

        def steady(eng, body):
            body(0, 0, True, False, True)
            body(1, 1, True, True, True)
            with eng.Fori(0, (B - 4) // 2) as m:
                body(m * 2 + 2, 0, True, True, True)
                body(m * 2 + 3, 1, True, True, True)
            body(B - 2, 0, True, True, True)
            body(B - 1, 1, True, True, False)
            body(B, 0, False, True, False)

        def known_positive(n, base):
            return not isinstance(n, int) or n >= base

        block = ctx.enter_context(nc.Block())

        @block.sync
        def _(sp):
            sp.dma_start(ident[:, :], ident_c).then_inc(weights_in, 16)
            sp.dma_start(w1[:, :, :], w_up1.rearrange("(h p) k a b -> p h (k a b)", p=P)).then_inc(weights_in, 16)
            sp.dma_start(wp[:, :, :], w_perc.rearrange("(c m) a y x -> c m (a y x)", m=3)).then_inc(weights_in, 16)
            sp.dma_start(bp[:, :], b_perc.rearrange("(c m) -> c m", m=3)).then_inc(weights_in, 16)
            sp.dma_start(x_in[:, 0, :, :], x_dram[0]).then_inc(x_loaded[0], 16)
            sp.dma_start(b1[:, :], b_up1.rearrange("(h p) -> p h", p=P), allow_slow_non_contiguous=True).then_inc(weights_in, 16)
            sp.dma_start(w2[:, :], w_up2.rearrange("c k a b -> c (k a b)")).then_inc(weights_in, 16)
            sp.dma_start(wqkv[:, :, :], w_qkv.rearrange("(j p) c -> p j c", p=P)).then_inc(weights_in, 16)
            sp.dma_start(b2[:, :], b_up2.rearrange("(p a) -> p a", a=1)).then_inc(weights_in, 16)
            sp.dma_start(bqk[:, :], b_qkv[0:2 * C].rearrange("(j p) -> p j", p=P), allow_slow_non_contiguous=True).then_inc(weights_in, 16)
            sp.dma_start(bv[:, :], b_qkv[2 * C:3 * C].partition_broadcast(P)).then_inc(weights_in, 16)
            sp.dma_start(mask_f[:, :, :], mask_c).then_inc(weights_in, 16)
            sp.dma_start(x_in[:, 1, :, :], x_dram[1]).then_inc(x_loaded[1], 16)

            def body(n, par, conv, attn, more):
                if conv and (not isinstance(n, int) or n + 2 < B):
                    sp.wait_ge(xt_ready, n * 2 + 2)
                    sp.dma_start(x_in[:, par, :, :], x_dram[n + 2]).then_inc(x_loaded[par], 16)
                if attn:
                    sp.wait_ge(v_done, n * 2)
                    sp.dma_start(v_halo[0:W, 1:T, :], v_sb[P - W:P, 0:T - 1, :]).then_inc(vh_done, 16)
                    sp.dma_start(v_halo[W:HALO, 0:T - 1, :], v_sb[0:W, 1:T, :]).then_inc(vh_done, 16)
                    for g in range(2):
                        sp.wait_ge(out_done, n * 2 - 1 + g)
                        sp.dma_start(out_dram[n - 1][:, g * 4:g * 4 + 4, :],
                                     out_sb[:, g * 4:g * 4 + 4, :]).then_inc(stored[g], 16)

            steady(sp, body)
            for g in range(2):
                sp.wait_ge(stored[g], 16 * B)

        @block.tensor
        def _(pe):
            pe.wait_ge(weights_in, 16 * N_W)
            for m in range(3):
                for g in range(2):
                    i = 2 * m + g
                    pe.transpose(bank[i // 4][:, (i % 4) * P:(i % 4 + 1) * P], w1[:, g, m:3 * C:3], ident[:, :])
            for g in range(2):
                pe.transpose(bank[6][:, g * P:(g + 1) * P], w2[:, g * P:(g + 1) * P], ident[:, :])
            for j in range(3):
                last = pe.transpose(bank[2][:, j * P:(j + 1) * P], wqkv[:, j, :], ident[:, :])
            last.then_inc(wt_ready, 1)
            pe.wait_ge(wt_copied, 3)
            for g in range(2):
                for m in range(3):
                    last = pe.matmul(bank[3][:, g:g + 1], w1T[:, m, g * P:(g + 1) * P], bp[:, m:m + 1],
                                     start=(m == 0), stop=(m == 2))
            last.then_inc(b1_ready, 1)

            def transpose_x(n, par):
                pe.wait_ge(x_loaded[par], n * 8 + (8 if par else 16))
                if known_positive(n, 2):
                    pe.wait_ge(v_done, n * 2 - 2)
                for c in range(NCH):
                    for t in range(4):
                        last = pe.transpose(bank[4 + c][:, t * P:(t + 1) * P], x_in[:, par, c * 4 + t, :], ident[:, :])
                    last.then_inc(xt_ready, 1)

            def conv_half(n, par, g, second):
                c, half = divmod(g, 2)
                if not second:
                    if g == 0:
                        pe.wait_ge(xhi_done, n * 2 + 2)
                        pe.wait_ge(xlo_done, n * 2 + 2)
                    if g >= 2 or known_positive(n, 1):
                        pe.wait_ge(hid_done, n * 4 + (g - 1))
                steps = [(tap, a, b) for tap in range(9) for a, b in ((whi, xhi), (whi, xlo), (wlo, xhi))]
                cut = 14
                for i, (tap, a, b) in list(enumerate(steps))[cut if second else 0:None if second else cut]:
                    dy, dx = TAPS[tap]
                    r = c * CR + dy
                    last = pe.matmul(bank[g % 2][:, :], a[:, tap, half * P:(half + 1) * P],
                                     b[:, par, r:r + CR, dx:dx + W], start=(i == 0), stop=(i == 26))
                if second:
                    last.then_inc(conv_ready, 1)

            def scores(n, j):
                if j >= 2 or known_positive(n, 2):
                    pe.wait_ge(p_done, n * 8 + (2 * j - 10))
                s = bank[2 + j % 2]
                kinds = 0 if j == 0 else 2 if j == T // 2 - 1 else 1
                pe.matmul(s[:, 0:2 * SC], ident_bf[:, :],
                          mask_bf[:, kinds:kinds + 2, :].rearrange("p a b -> p (a b)"), start=True, stop=False,
                          skip_group_check=True)
                rows = k_sb[:, :].rearrange("p (r w) -> p r w", w=W)
                for u in range(2):
                    t = 2 * j + u
                    o = u * SC
                    qt = q_sb[:, t * P:(t + 1) * P]
                    pe.matmul(s[:, o:o + P], qt, k_sb[:, t * P:(t + 1) * P], start=False, stop=False,
                              skip_group_check=True)
                    lo, hi = (1 if t == 0 else 0), (1 if t == T - 1 else 2)
                    first = TR * t - 1 if lo == 0 else TR * t + TR
                    last = pe.matmul(s[:, o + P + lo * W:o + P + hi * W], qt,
                                     rows[:, first:first + (TR + 1) * (hi - lo - 1) + 1:TR + 1, :],
                                     start=False, stop=(u == 1), skip_group_check=True)
                last.then_inc(s_ready, 1)

            def transpose_p(n, g):
                pe.wait_ge(p_done, n * 8 + (4 * g - 4))
                if g == 0:
                    if not (isinstance(n, int) and n >= B - 0):
                        pass
                else:
                    pe.wait_ge(ptm_done, n * 2 - 1)
                    pe.wait_ge(pth_done, n * 2 - 1)
                for u in range(4):
                    pe.transpose(bank[4][:, u * P:(u + 1) * P], p_sb[:, 4 * g + u, 0:P], ident[:, :])
                for u in range(4):
                    last = pe.transpose(bank[5][0:HALO, u * P:(u + 1) * P], p_sb[:, 4 * g + u, P:P + HALO],
                                        ident[:, :])
                last.then_inc(pt_ready, 1)

            def transpose_h(n, g):
                if g == 1:
                    pe.wait_ge(out_done, n * 2 - 1)
                for u in range(4):
                    last = pe.transpose(bank[7][:, u * P:(u + 1) * P], h[:, (4 * g + u) * P:(4 * g + u + 1) * P],
                                        ident[:, :])
                last.then_inc(hp_ready, 1)

            def values(n, g):
                pe.wait_ge(ptm_done, n * 2 + (g - 1))
                pe.wait_ge(pth_done, n * 2 + (g - 1))
                if g == 0:
                    pe.wait_ge(vh_done, n * 32)
                for u in range(4):
                    t = 4 * g + u
                    pe.matmul(bank[6][:, u * P:(u + 1) * P], pt_main[:, t, :], v_sb[:, t, :], start=True, stop=False)
                    last = pe.matmul(bank[6][:, u * P:(u + 1) * P], pt_halo[:, t, :], v_halo[:, t, :], start=False,
                                     stop=True)
                last.then_inc(o_ready, 1)

            def body(n, par, conv, attn, more):
                a = n - 1
                if conv:
                    if isinstance(n, int) and n == 0:
                        transpose_x(0, 0)
                        pe.wait_ge(whi_done, 1)
                        pe.wait_ge(wlo_done, 1)
                    conv_half(n, par, 0, False)
                if attn:
                    if isinstance(n, int) and n == 1:
                        pe.wait_ge(consts_done, 5)
                    pe.wait_ge(hid_done, n * 4)
                    for c in range(NCH):
                        for half in range(2):
                            last = pe.matmul(bank[4 + c][:, :], w2T[:, half, :], hid[:, half, c * CH:(c + 1) * CH],
                                             start=(half == 0), stop=(half == 1))
                        last.then_inc(up_ready, 1)
                if conv:
                    conv_half(n, par, 0, True)
                    conv_half(n, par, 1, False)
                if attn:
                    for c in range(NCH):
                        pe.wait_ge(h_done, n * 2 + (c - 1))
                        pe.matmul(bank[4 + c][:, :], wqkvT[:, 0, :], h[:, c * CH:(c + 1) * CH], start=True,
                                  stop=True).then_inc(q_ready, 1)
                    if known_positive(n, 2):
                        pe.wait_ge(out_done, n * 2 - 2)
                    for c in range(NCH):
                        pe.matmul(bank[6 + c][:, :], wqkvT[:, 1, :], h[:, c * CH:(c + 1) * CH], start=True,
                                  stop=True).then_inc(k_ready, 1)
                if conv:
                    conv_half(n, par, 1, True)
                if attn:
                    for g in range(2):
                        pe.wait_ge(q_done, n * 2 + (g - 1))
                        for u in range(4):
                            t = 4 * g + u
                            last = pe.matmul(bank[4 + g][:, u * P:(u + 1) * P], h[:, t * P:(t + 1) * P],
                                             wqkvT[:, 2, :], start=True, stop=True)
                        last.then_inc(v_ready, 1)
                    pe.wait_ge(k_done, n * 2)
                    scores(n, 0)
                    scores(n, 1)
                if conv:
                    conv_half(n, par, 2, False)
                if more:
                    transpose_x(n + 1, 1 - par)
                if attn:
                    scores(n, 2)
                    scores(n, 3)
                if conv:
                    conv_half(n, par, 2, True)
                if attn:
                    if more:
                        pe.wait_ge(xlo_done, n * 2 + 4)
                    else:
                        pe.wait_ge(v_done, n * 2)
                    transpose_p(n, 0)
                if conv:
                    conv_half(n, par, 3, False)
                if attn:
                    transpose_h(n, 0)
                    values(n, 0)
                    transpose_p(n, 1)
                if conv:
                    conv_half(n, par, 3, True)
                if attn:
                    transpose_h(n, 1)
                    values(n, 1)

            steady(pe, body)

        @block.scalar
        def _(act):
            act.wait_ge(weights_in, 16 * N_W)
            nc.scalar.mul(bq_s[:, :], bqk[:, 0:1], SCALE).then_inc(consts_done, 1)
            nc.scalar.copy(ident_bf[:, :], ident[:, :]).then_inc(consts_done, 1)
            nc.scalar.copy(mask_bf[:, :, :], mask_f[:, :, :]).then_inc(consts_done, 1)
            act.wait_ge(wt_ready, 1)
            nc.scalar.copy(w2T[:, :, :], bank[6][:, 0:2 * P].rearrange("p (h c) -> p h c", h=2)).then_inc(consts_done, 1)
            nc.scalar.copy(wqkvT[:, :, :], bank[2][:, 0:3 * P].rearrange("p (h c) -> p h c", h=3)).then_inc(consts_done, 1)
            act.wait_ge(setup_dve, 27)
            nc.scalar.copy(whi[:, :, :], weff[:, :, :]).then_inc(whi_done, 1)

            def high_x(n, par):
                for c in range(NCH):
                    act.wait_ge(xt_ready, n * 2 + (c + 1))
                    if known_positive(n, 2):
                        act.wait_ge(h_done, n * 2 - 2)
                    nc.scalar.copy(xhi[:, par, 1 + c * CR:1 + (c + 1) * CR, 1:W + 1],
                                   bank[4 + c][:, :].rearrange("p (r w) -> p r w", w=W)).then_inc(xhi_done, 1)

            def gelu(n, g):
                c, half = divmod(g, 2)
                act.wait_ge(conv_ready, n * 4 + (g + 1))
                nc.scalar.activation(hid[:, half, c * CH:(c + 1) * CH], bank[g % 2][:, :], ACT.Gelu,
                                     bias=b1eff[:, half:half + 1]).then_inc(hid_done, 1)

            def body(n, par, conv, attn, more):
                if isinstance(n, int) and n == 0:
                    act.wait_ge(zeroed, 2)
                    high_x(0, 0)
                    act.wait_ge(setup_dve, 28)
                if attn and not conv:
                    pass
                if conv:
                    gelu(n, 0)
                if attn:
                    if isinstance(n, int) and n == 1:
                        act.wait_ge(consts_done, 5)
                    for c in range(NCH):
                        act.wait_ge(q_ready, n * 2 + (c - 1))
                        nc.scalar.activation(q_sb[:, c * CH:(c + 1) * CH], bank[4 + c][:, :], ACT.Identity,
                                             bias=bq_s[:, :], scale=SCALE).then_inc(q_done, 1)
                if conv:
                    gelu(n, 1)

                def exp(t):
                    if t % 2 == 0:
                        act.wait_ge(max_done, n * 4 + (t // 2 - 3))
                    s = bank[2 + (t // 2) % 2]
                    nc.scalar.activation(p_sb[:, t, :], s[:, (t % 2) * SC:(t % 2 + 1) * SC], ACT.Exp,
                                         bias=negmax[:, t:t + 1], accum_out=psum_p[:, t:t + 1]).then_inc(p_done, 1)

                if attn:
                    for t in range(4):
                        exp(t)
                if more:
                    high_x(n + 1, 1 - par)
                if attn:
                    for t in range(4, T):
                        exp(t)
                if conv:
                    gelu(n, 2)
                if attn:
                    for g in range(2):
                        act.wait_ge(pt_ready, n * 2 + (g - 1))
                        nc.scalar.copy(pt_main[:, 4 * g:4 * g + 4, :],
                                       bank[4][:, :].rearrange("p (t q) -> p t q", t=4)).then_inc(ptm_done, 1)
                if conv:
                    gelu(n, 3)

            steady(act, body)

        @block.vector
        def _(dve):
            dve.wait_ge(wt_ready, 1)
            nc.vector.tensor_copy(w1T[:, 0, :], bank[0][:, 0:HID]).then_inc(wt_copied, 1)
            nc.vector.tensor_copy(w1T[:, 1, :], bank[0][:, HID:2 * HID]).then_inc(wt_copied, 1)
            nc.vector.tensor_copy(w1T[:, 2, :], bank[1][:, 0:HID]).then_inc(wt_copied, 1)
            dve.wait_ge(wt_copied, 3)
            for tap in range(9):
                nc.vector.tensor_scalar(weff[:, tap, :], w1T[:, 0, :], wp[:, 0, tap:tap + 1], None,
                                        ALU.mult).then_inc(setup_dve, 1)
            for m in (1, 2):
                for tap in range(9):
                    dve.wait_ge(setup_dve, 9 * (m - 1) + tap + 1)
                    nc.vector.scalar_tensor_tensor(out=weff[:, tap, :], in0=w1T[:, m, :],
                                                   scalar=wp[:, m, tap:tap + 1], in1=weff[:, tap, :], op0=ALU.mult,
                                                   op1=ALU.add).then_inc(setup_dve, 1)
            dve.wait_ge(b1_ready, 1)
            nc.vector.tensor_tensor(b1eff[:, :], bank[3][:, 0:2], b1[:, :], ALU.add).then_inc(setup_dve, 1)
            dve.wait_ge(whi_done, 1)
            nc.vector.tensor_tensor(wlo[:, :, :], weff[:, :, :], whi[:, :, :].bitcast(F32),
                                    ALU.subtract).then_inc(wlo_done, 1)

            def low_x(n, par):
                for c in range(NCH):
                    dve.wait_ge(xhi_done, n * 2 + (c + 1))
                    rows = slice(1 + c * CR, 1 + (c + 1) * CR)
                    nc.vector.tensor_tensor(xlo[:, par, rows, 1:W + 1],
                                            bank[4 + c][:, :].rearrange("p (r w) -> p r w", w=W),
                                            xhi[:, par, rows, 1:W + 1].bitcast(F32),
                                            ALU.subtract).then_inc(xlo_done, 1)

            def row_max(n, j):
                dve.wait_ge(s_ready, n * 4 + (j - 3))
                nc.vector.tensor_reduce(negmax[:, 2 * j:2 * j + 2],
                                        bank[2 + j % 2][:, 0:2 * SC].rearrange("p (a b) -> p a b", a=2), AX.X,
                                        ALU.max, negate=True).then_inc(max_done, 1)

            def body(n, par, conv, attn, more):
                if isinstance(n, int) and n == 0:
                    low_x(0, 0)
                if attn:
                    res = 1 - par
                    for c in range(NCH):
                        rows = slice(1 + c * CR, 1 + (c + 1) * CR)
                        dve.wait_ge(up_ready, n * 2 + (c - 1))
                        nc.vector.scalar_tensor_tensor(
                            out=h[:, c * CH:(c + 1) * CH].rearrange("p (r w) -> p r w", w=W),
                            in0=bank[4 + c][:, :].rearrange("p (r w) -> p r w", w=W), scalar=b2[:, 0:1],
                            in1=xhi[:, res, rows, 1:W + 1].bitcast(F32), op0=ALU.add,
                            op1=ALU.add).then_inc(hx_done, 1)
                    for c in range(NCH):
                        dve.wait_ge(k_ready, n * 2 + (c - 1))
                        nc.vector.tensor_scalar(k_sb[:, c * CH:(c + 1) * CH], bank[6 + c][:, :], bqk[:, 1:2], None,
                                                ALU.add).then_inc(k_done, 1)
                    for g in range(2):
                        dve.wait_ge(v_ready, n * 2 + (g - 1))
                        nc.vector.tensor_tensor(v_sb[:, 4 * g:4 * g + 4, :],
                                                bank[4 + g][:, :].rearrange("p (t c) -> p t c", t=4),
                                                bv[:, :].unsqueeze(1).to_broadcast([P, 4, C]),
                                                ALU.add).then_inc(v_done, 1)
                    row_max(n, 0)
                    row_max(n, 1)
                if more:
                    low_x(n + 1, 1 - par)
                if attn:
                    row_max(n, 2)
                    row_max(n, 3)
                    for g in range(2):
                        dve.wait_ge(pt_ready, n * 2 + (g - 1))
                        nc.vector.tensor_copy(pt_halo[:, 4 * g:4 * g + 4, :],
                                              bank[5][0:HALO, :].rearrange("p (t q) -> p t q", t=4)).then_inc(pth_done, 1)
                        if g == 0:
                            dve.wait_ge(p_done, n * 8)
                            nc.vector.reciprocal(rsum[:, :], psum_p[:, :]).then_inc(rsum_done, 1)
                            dve.wait_ge(rsum_done, n)
                        dve.wait_ge(o_ready, n * 2 + (g - 1))
                        nc.vector.tensor_tensor(o_sb[:, 4 * g:4 * g + 4, :],
                                                bank[6][:, :].rearrange("p (t c) -> p t c", t=4),
                                                rsum[:, 4 * g:4 * g + 4].unsqueeze(2).to_broadcast([P, 4, C]),
                                                ALU.mult).then_inc(om_done, 1)
                        dve.wait_ge(om_done, n * 2 + (g - 1))
                        dve.wait_ge(hp_ready, n * 2 + (g - 1))
                        if known_positive(n, 2):
                            dve.wait_ge(stored[g], n * 16 - 16)
                        nc.vector.tensor_tensor(out_sb[:, 4 * g:4 * g + 4, :], o_sb[:, 4 * g:4 * g + 4, :],
                                                bank[7][:, :].rearrange("p (t c) -> p t c", t=4),
                                                ALU.add).then_inc(out_done, 1)

            steady(dve, body)

        @block.gpsimd
        def _(pool):
            nc.gpsimd.memset(xhi[:, :, :, :].bitcast(F32), 0.0).then_inc(zeroed, 1)
            nc.gpsimd.memset(xlo[:, :, :, :].bitcast(F32), 0.0).then_inc(zeroed, 1)
            nc.gpsimd.memset(v_halo[:, :, :], 0.0).then_inc(zeroed, 1)

            def body(n, par, conv, attn, more):
                if attn:
                    for c in range(NCH):
                        rows = slice(1 + c * CR, 1 + (c + 1) * CR)
                        pool.wait_ge(hx_done, n * 2 + (c - 1))
                        hc = h[:, c * CH:(c + 1) * CH].rearrange("p (r w) -> p r w", w=W)
                        nc.gpsimd.tensor_tensor(hc, hc, xlo[:, 1 - par, rows, 1:W + 1].bitcast(F32),
                                                ALU.add).then_inc(h_done, 1)

            steady(pool, body)


_INS = ["x", "L0_conv_w_perc", "L0_conv_b_perc", "L0_conv_w_up1", "L0_conv_b_up1", "L0_conv_w_up2",
        "L0_conv_b_up2", "L0_conv_w_qkv", "L0_conv_b_qkv"]


def kernel(**inputs):
    import concourse.bacc as bacc
    from concourse.bass_utils import run_bass_kernel_spmd as run

    nc = bacc.Bacc("TRN2", target_bir_lowering=False, num_devices=1)
    arrays = {name: np.ascontiguousarray(inputs[name]) for name in _INS}
    arrays["identity"] = np.eye(P, dtype=np.float32)
    arrays["masks"] = window_masks()
    args = [nc.dram_tensor(name, a.shape, mybir.dt.from_np(a.dtype), kind="ExternalInput").ap()
            for name, a in arrays.items()]
    out = nc.dram_tensor("out", (B, H, W, C), F32, kind="ExternalOutput").ap()
    build(nc, *args, out)
    r = run(nc, [arrays], core_ids=[0])
    return r.results[0]["out"]
```

```python
from contextlib import ExitStack

import numpy as np

import concourse.bass as bass
from concourse import mybir
from concourse.alu_op_type import AluOpType as ALU

ACT = mybir.ActivationFunctionType
AX = mybir.AxisListType
F32 = mybir.dt.float32
F32R = mybir.dt.float32r
BF16 = mybir.dt.bfloat16

P = 128
B, H, W, C = 16, 32, 32, 128
PIX = H * W
TR = P // W
T = H // TR
CH = 512
NCH = PIX // CH
HID = 2 * C
WINDOW = P + 2 * W
REST = WINDOW - P
NPAD = 6
SC = WINDOW + NPAD
NEG = -1e30
SCALE = float(C) ** -0.5

K4 = 4
WIN = W // K4
S = H * WIN
NJ = 6
TS = (H + 2) * WIN
PLANES = (0, 3, 1, 2)
M_PLACE = {1: (0, 0), 3: (0, S), 2: (1, 0), 4: (1, S), 0: (2, 0), 5: (2, S)}
M_ORDER = (1, 3, 2, 4, 0, 5)


def window_masks(dtype):
    m = np.full((P, 4, SC), NEG, dtype)
    for kind in range(4):
        for qy in range(TR):
            for qx in range(W):
                q = qy * W + qx
                inside = 0
                for ky in range(-1, TR + 1):
                    if abs(ky - qy) > 1 or (kind == 0 and ky < 0) or (kind == 3 and ky >= TR):
                        continue
                    for kx in range(max(0, qx - 1), min(W, qx + 2)):
                        m[q, kind, (ky + 1) * W + kx] = 0.0
                        inside += 1
                m[q, kind, WINDOW:WINDOW + 9 - inside] = 0.0
    return m


def build(nc, x, w_perc, b_perc, w_up1, b_up1, w_up2, b_up2, w_qkv, b_qkv, ident_c, ident_bf_c, mask_c, out):
    with ExitStack() as ctx:
        def sb(name, shape, dt=F32):
            return ctx.enter_context(nc.sbuf_tensor(name, shape, dt))

        def sem(name):
            return ctx.enter_context(nc.semaphore(name))

        def psum(name, banks):
            return ctx.enter_context(nc.psum_tensor(name, [P, banks, CH], F32))

        m_ps = psum("m_ps", 3)
        s_ps = psum("s_ps", 2)
        work = psum("work", 3)

        ident = sb("ident", [P, P])
        ident_bf = sb("ident_bf", [P, P], BF16)
        mask_bf = sb("mask_bf", [P, 4, SC], BF16)
        wp = sb("wp", [P, 3, 3, 3])
        bp = sb("bp", [P, 3])
        b1 = sb("b1", [P, 2])
        b2 = sb("b2", [P, 1])
        bqk = sb("bqk", [P, 2])
        bv = sb("bv", [P, C])
        w1T = sb("w1T", [P, 3, HID])
        w2T = sb("w2T", [P, 2 * C])
        w2hi = sb("w2hi", [P, 2 * C], F32R)
        w2lo = sb("w2lo", [P, 2 * C], F32R)
        wqkvT = sb("wqkvT", [P, 3 * C])
        wqhi = sb("wqhi", [P, 3 * C], F32R)
        wqlo = sb("wqlo", [P, 3 * C], F32R)
        b1eff = sb("b1eff", [P, 2])
        bq_s = sb("bq_s", [P, 1])
        wg = sb("wg", [P, NJ, 3, 3])
        gt = sb("gt", [P, 4, 3, 3])
        weff = sb("weff", [P, 2, 3, HID])
        whi = sb("whi", [P, NJ, 3, HID], F32R)
        wlo = sb("wlo", [P, NJ, 3, HID], F32R)

        x_in = sb("x_in", [P, 2, 2, K4, C])
        xp = sb("xp", [P, 2, K4, H + 2, WIN + 2])
        fc = sb("fc", [P, 2, TS])
        ge = sb("ge", [P, 2, TS])
        ab = sb("ab", [P, 2, TS])
        t = sb("t", [P, NJ, TS])
        thi = sb("thi", [P, 2, NJ, TS], F32R)
        tlo = sb("tlo", [P, 2, NJ, TS], F32R)
        m13 = sb("m13", [P, CH])
        ps_sb = sb("ps_sb", [P, CH])
        ru_sb = sb("ru_sb", [P, CH])
        y = sb("y", [P, 2, K4, S])
        hid = sb("hid", [P, 2, PIX])
        hid_hi = sb("hid_hi", [P, 2, PIX], F32R)
        hid_lo = sb("hid_lo", [P, 2, PIX], F32R)
        h_around = sb("h_around", [P, W + PIX + W])
        h = h_around[:, W:W + PIX]
        h_hi = sb("h_hi", [P, PIX], F32R)
        h_lo = sb("h_lo", [P, PIX], F32R)
        q_sb = sb("q_sb", [P, PIX])
        k_sb = sb("k_sb", [P, PIX])
        v_sb = sb("v_sb", [P, T + 1, C])
        negmax = sb("negmax", [P, T])
        p_sum = sb("p_sum", [P, T])
        rsum = sb("rsum", [P, T])
        p_sb = sb("p_sb", [P, T, SC])
        pt_main = sb("pt_main", [P, T, P])
        pt_rest = sb("pt_rest", [REST, T, P])
        out_sb = sb("out_sb", [P, T, C])

        w1 = y[:, :, :, :].rearrange("p h k s -> p h (k s)")[:, :, 0:3 * C]
        wqkv = h[:, 0:3 * C].rearrange("p (j c) -> p j c", j=3)
        w2 = h[:, 3 * C:3 * C + HID]

        first_in = sem("first_in")
        filters_in = sem("filters_in")
        weights_in = sem("weights_in")
        x_loaded = [sem(f"x_loaded{i}") for i in range(2)]
        stored = [sem(f"stored{i}") for i in range(2)]
        zeroed = sem("zeroed")
        w1t_ready = sem("w1t_ready")
        wt_ready = sem("wt_ready")
        w1t_copied = sem("w1t_copied")
        wt_copied = sem("wt_copied")
        b1_ready = sem("b1_ready")
        b1_done = sem("b1_done")
        filters_done = sem("filters_done")
        weff0_done = sem("weff0_done")
        weff_done = sem("weff_done")
        whi_done = sem("whi_done")
        wlo_done = sem("wlo_done")
        consts_done = sem("consts_done")
        small_hi_done = sem("small_hi_done")
        small_lo_done = sem("small_lo_done")
        xt_ready = sem("xt_ready")
        m_ready = sem("m_ready")
        up_ready = sem("up_ready")
        q_ready = sem("q_ready")
        k_ready = sem("k_ready")
        v_ready = sem("v_ready")
        s_ready = sem("s_ready")
        pt_ready = sem("pt_ready")
        hp_ready = sem("hp_ready")
        o_ready = sem("o_ready")
        x_done = sem("x_done")
        thi_done = sem("thi_done")
        m13_done = sem("m13_done")
        hid_done = sem("hid_done")
        q_done = sem("q_done")
        k_done = sem("k_done")
        ptr_done = sem("ptr_done")
        p_done = sem("p_done")
        ptm_done = sem("ptm_done")
        ab_done = sem("ab_done")
        td_done = sem("td_done")
        ps_done = sem("ps_done")
        ru_done = sem("ru_done")
        y_part_done = sem("y_part_done")
        y_done = sem("y_done")
        hid_hi_done = sem("hid_hi_done")
        h_done = sem("h_done")
        h_hi_done = sem("h_hi_done")
        h_lo_done = sem("h_lo_done")
        v_done = sem("v_done")
        max_done = sem("max_done")
        rsum_done = sem("rsum_done")
        om_done = sem("om_done")
        out_done = sem("out_done")
        fcge_done = sem("fcge_done")
        tp_done = sem("tp_done")
        tlo_done = sem("tlo_done")
        hid_lo_done = sem("hid_lo_done")

        x_dram = x.rearrange("b (g r) (w k) c -> b (r w) g k c", g=2, k=K4)
        out_dram = out.rearrange("b (t r) w c -> b (r w) t c", r=TR)
        N_W = 6

        def steady(eng, body):
            body(0, 0, True, False, True)
            body(1, 1, True, True, True)
            with eng.Fori(0, (B - 4) // 2) as m:
                body(m * 2 + 2, 0, True, True, True)
                body(m * 2 + 3, 1, True, True, True)
            body(B - 2, 0, True, True, True)
            body(B - 1, 1, True, True, False)
            body(B, 0, False, True, False)

        def from_image(n, base):
            return not isinstance(n, int) or n >= base

        block = ctx.enter_context(nc.Block())

        @block.sync
        def _(sp):
            def load(dst, src, **kw):
                sp.dma_start(dst, src, **kw).then_inc(weights_in, 16)

            sp.dma_start(ident[:, :], ident_c).then_inc(first_in, 16)
            sp.dma_start(w1, w_up1.rearrange("(h p) k a b -> p h (k a b)", p=P)).then_inc(first_in, 16)
            sp.dma_start(x_in[:, 0, :, :, :], x_dram[0]).then_inc(x_loaded[0], 16)
            load(w2, w_up2.rearrange("c k a b -> c (k a b)"))
            load(wqkv, w_qkv.rearrange("(j p) c -> p j c", p=P))
            load(bqk[:, :], b_qkv[0:2 * C].rearrange("(j p) -> p j", p=P), allow_slow_non_contiguous=True)
            load(bv[:, :], b_qkv[2 * C:3 * C].partition_broadcast(P))
            load(mask_bf[:, :, :], mask_c)
            load(ident_bf[:, :], ident_bf_c)
            sp.dma_start(x_in[:, 1, :, :, :], x_dram[1]).then_inc(x_loaded[1], 16)

            def body(n, par, conv, attn, more):
                if conv and (not isinstance(n, int) or n + 2 < B):
                    sp.wait_ge(xt_ready, n + 1)
                    sp.dma_start(x_in[:, par, :, :, :], x_dram[n + 2]).then_inc(x_loaded[par], 16)
                if attn:
                    for g in range(2):
                        sp.wait_ge(out_done, n * 2 - 1 + g)
                        sp.dma_start(out_dram[n - 1][:, g * 4:g * 4 + 4, :],
                                     out_sb[:, g * 4:g * 4 + 4, :]).then_inc(stored[g], 16)

            steady(sp, body)
            for g in range(2):
                sp.wait_ge(stored[g], 16 * B)

        @block.tensor
        def _(pe):
            pe.wait_ge(first_in, 32)
            for m in range(3):
                for g in range(2):
                    last = pe.transpose(m_ps[:, m, g * P:(g + 1) * P], w1[:, g, m:3 * C:3], ident[:, :])
            last.then_inc(w1t_ready, 1)

            def small_weights():
                pe.wait_ge(weights_in, 16 * N_W)
                for g in range(2):
                    pe.transpose(work[:, 0, g * P:(g + 1) * P], w2[:, g * P:(g + 1) * P], ident[:, :])
                for j in range(3):
                    last = pe.transpose(work[:, 1, j * P:(j + 1) * P], wqkv[:, j, :], ident[:, :])
                last.then_inc(wt_ready, 1)
                pe.wait_ge(filters_in, 64)
                pe.wait_ge(w1t_copied, 3)
                for g in range(2):
                    for m in range(3):
                        last = pe.matmul(work[:, 2, g:g + 1], w1T[:, m, g * P:(g + 1) * P], bp[:, m:m + 1],
                                         start=(m == 0), stop=(m == 2))
                last.then_inc(b1_ready, 1)

            def transpose_x(n, par):
                pe.wait_ge(x_loaded[par], n * 8 + (8 if par else 16))
                for k in range(K4):
                    for g in range(2):
                        i = 2 * k + g
                        last = pe.transpose(s_ps[:, i // 4, (i % 4) * P:(i % 4 + 1) * P], x_in[:, par, g, k, :],
                                            ident[:, :])
                last.then_inc(xt_ready, 1)

            def unit(n, par, i):
                half, i = divmod(i, NJ)
                j = M_ORDER[i]
                b, col = M_PLACE[j]
                if half == 0 and i == 0:
                    pe.wait_ge(thi_done, n + 1)
                    pe.wait_ge(tlo_done, n + 1)
                if col == 0 and (half == 1 or from_image(n, 1)):
                    pe.wait_ge((m13_done, ru_done, y_done)[b], n * 2 + half)
                if isinstance(n, int) and n == 0 and half == 0:
                    pe.wait_ge(wlo_done, i + 1)
                steps = [(dy, a, c) for dy in range(3) for a, c in ((whi, thi), (whi, tlo), (wlo, thi))]
                for s, (dy, a, c) in enumerate(steps):
                    last = pe.matmul(m_ps[:, b, col:col + S], a[:, j, dy, half * P:(half + 1) * P],
                                     c[:, par, j, dy * WIN:dy * WIN + S], start=(s == 0), stop=(s == len(steps) - 1))
                if col:
                    last.then_inc(m_ready, 1)

            def up(n, c):
                pe.wait_ge(hid_lo_done, n * 4 + (c - 1))
                i = 0
                for half in range(2):
                    for a, b in ((w2hi, hid_hi), (w2hi, hid_lo), (w2lo, hid_hi)):
                        last = pe.matmul(work[:, c, :], a[:, half * C:(half + 1) * C],
                                         b[:, half, c * CH:(c + 1) * CH], start=(i == 0), stop=(i == 5))
                        i += 1
                last.then_inc(up_ready, 1)

            def project(j, c, b, ready):
                w = slice(j * C, (j + 1) * C)
                cols = slice(c * CH, (c + 1) * CH)
                pe.matmul(work[:, b, :], wqhi[:, w], h_hi[:, cols], start=True, stop=False)
                pe.matmul(work[:, b, :], wqhi[:, w], h_lo[:, cols], start=False, stop=False)
                pe.matmul(work[:, b, :], wqlo[:, w], h_hi[:, cols], start=False, stop=True).then_inc(ready, 1)

            def project_v(g, b):
                tiles = range(4 * g, 4 * g + 4) if g < 2 else [T]
                for u, i in enumerate(tiles):
                    rows = P if g < 2 else REST
                    last = pe.matmul(work[0:rows, b, u * P:(u + 1) * P], h_around[:, i * P:i * P + rows],
                                     wqkvT[:, 2 * C:3 * C], start=True, stop=True)
                last.then_inc(v_ready, 1)

            def scores(n, j):
                if j >= 2:
                    pe.wait_ge(p_done, n * 8 + (2 * j - 10))
                s = s_ps[:, j % 2, :]
                kinds = 0 if j == 0 else 2 if j == T // 2 - 1 else 1
                pe.matmul(s[:, 0:2 * SC], ident_bf[:, :],
                          mask_bf[:, kinds:kinds + 2, :].rearrange("p a b -> p (a b)"), start=True, stop=False,
                          skip_group_check=True)
                for u in range(2):
                    i = 2 * j + u
                    first, end = (W if i == 0 else 0), (WINDOW - W if i == T - 1 else WINDOW)
                    last = pe.matmul(s[:, u * SC + first:u * SC + end], q_sb[:, i * P:(i + 1) * P],
                                     k_sb[:, i * P - W + first:i * P - W + end], start=False, stop=(u == 1),
                                     skip_group_check=True)
                last.then_inc(s_ready, 1)

            def transpose_p(n, g):
                pe.wait_ge(p_done, n * 8 + (4 * g - 4))
                main = work[:, 2 if g == 0 else 0, :]
                rest = work[0:REST, 0, :] if g == 0 else s_ps[0:REST, 0, :]
                if g == 0:
                    pe.wait_ge(v_done, n * 3)
                else:
                    pe.wait_ge(ptr_done, n * 2 - 1)
                for u in range(4):
                    pe.transpose(main[:, u * P:(u + 1) * P], p_sb[:, 4 * g + u, 0:P], ident[:, :])
                for u in range(4):
                    last = pe.transpose(rest[:, u * P:(u + 1) * P], p_sb[:, 4 * g + u, P:WINDOW], ident[:, :])
                last.then_inc(pt_ready, 1)

            def transpose_h(n, g):
                dst = work[:, 1, :] if g == 0 else s_ps[:, 1, :]
                for u in range(4):
                    last = pe.transpose(dst[:, u * P:(u + 1) * P], h[:, (4 * g + u) * P:(4 * g + u + 1) * P],
                                        ident[:, :])
                last.then_inc(hp_ready, 1)

            def values(n, g):
                pe.wait_ge(ptm_done, n * 2 + (g - 1))
                pe.wait_ge(ptr_done, n * 2 + (g - 1))
                dst = work[:, 2 if g == 0 else 0, :]
                for u in range(4):
                    i = 4 * g + u
                    pe.matmul(dst[:, u * P:(u + 1) * P], pt_main[:, i, :], v_sb[:, i, :], start=True, stop=False)
                    last = pe.matmul(dst[:, u * P:(u + 1) * P], pt_rest[:, i, :], v_sb[0:REST, i + 1, :], start=False,
                                     stop=True)
                last.then_inc(o_ready, 1)

            def body(n, par, conv, attn, more):
                def units(*which):
                    if conv:
                        for i in which:
                            unit(n, par, i)

                if isinstance(n, int) and n == 0:
                    transpose_x(0, 0)
                    small_weights()
                units(0, 1, 2, 3)
                if isinstance(n, int) and n == 1:
                    pe.wait_ge(small_lo_done, 2)
                    pe.wait_ge(zeroed, 3)
                if attn:
                    if from_image(n, 2):
                        pe.wait_ge(out_done, n * 2 - 2)
                    up(n, 0)
                    up(n, 1)
                units(4, 5)
                if more:
                    transpose_x(n + 1, 1 - par)
                if attn:
                    pe.wait_ge(h_lo_done, n * 2 - 1)
                    project(0, 0, 2, q_ready)
                    pe.wait_ge(h_lo_done, n * 2)
                    project(0, 1, 0, q_ready)
                    project(1, 0, 1, k_ready)
                    pe.wait_ge(q_done, n * 2 - 1)
                    project(1, 1, 2, k_ready)
                    pe.wait_ge(q_done, n * 2)
                    project_v(0, 0)
                    pe.wait_ge(k_done, n * 2 - 1)
                    project_v(1, 1)
                units(6)
                if attn:
                    pe.wait_ge(k_done, n * 2)
                    project_v(2, 2)
                    if more:
                        pe.wait_ge(x_done, n + 2)
                    scores(n, 0)
                    scores(n, 1)
                units(7, 8)
                if attn:
                    scores(n, 2)
                units(9)
                if attn:
                    scores(n, 3)
                    transpose_p(n, 0)
                units(10)
                if attn:
                    transpose_h(n, 0)
                    transpose_p(n, 1)
                    values(n, 0)
                units(11)
                if attn:
                    transpose_h(n, 1)
                    values(n, 1)

            steady(pe, body)

        @block.scalar
        def _(act):
            act.dma_start(wp[:, :, :, :], w_perc.rearrange("(c m) a y x -> c m (a y) x", m=3)).then_inc(filters_in, 16)
            act.dma_start(bp[:, :], b_perc.rearrange("(c m) -> c m", m=3)).then_inc(filters_in, 16)
            act.dma_start(b1[:, :], b_up1.rearrange("(h p) -> p h", p=P),
                          allow_slow_non_contiguous=True).then_inc(filters_in, 16)
            act.dma_start(b2[:, :], b_up2.rearrange("(p a) -> p a", a=1)).then_inc(filters_in, 16)

            def spread_x(n, par):
                act.wait_ge(xt_ready, n + 1)
                if from_image(n, 2):
                    act.wait_ge(h_done, n * 4 - 4)
                nc.scalar.copy(xp[:, par, :, 1:H + 1, 1:WIN + 1],
                               s_ps[:, :, :].rearrange("p a (b r w) -> p (a b) r w", b=2, w=WIN)).then_inc(x_done, 1)

            def high_t(n, par):
                act.wait_ge(td_done, n * 4 + 4)
                act.wait_ge(tp_done, n * 2 + 2)
                nc.scalar.copy(thi[:, par, :, :], t[:, :, :]).then_inc(thi_done, 1)

            def take_m13(n, half):
                act.wait_ge(m_ready, n * 6 + (3 * half + 1))
                if half or from_image(n, 1):
                    act.wait_ge(ru_done, n * 2 + half)
                nc.scalar.copy(m13[:, :], m_ps[:, 0, :]).then_inc(m13_done, 1)

            def gelu(n, half):
                act.wait_ge(y_part_done, n * 8 + (4 * half + 4))
                act.wait_ge(y_done, n * 2 + (half + 1))
                if from_image(n, 1):
                    act.wait_ge(hid_lo_done, n * 4 + (2 * half - 2))
                nc.scalar.activation(hid[:, half, :], y[:, half, :, :].rearrange("p k s -> p (k s)"), ACT.Gelu,
                                     bias=b1eff[:, half:half + 1]).then_inc(hid_done, 1)

            def first_products(i):
                if i >= 2:
                    act.wait_ge(wlo_done, i - 1)
                for dy in range(3):
                    nc.scalar.activation(weff[:, i % 2, dy, :], w1T[:, 0, :], ACT.Copy,
                                         scale=wg[:, M_ORDER[i], 0, dy:dy + 1]).then_inc(weff0_done, 1)

            act.wait_ge(w1t_copied, 1)
            act.wait_ge(filters_done, 11)
            first_products(0)
            act.wait_ge(zeroed, 1)
            spread_x(0, 0)
            first_products(1)
            for i, j in enumerate(M_ORDER):
                act.wait_ge(weff_done, 6 * (i + 1))
                nc.scalar.copy(whi[:, j, :, :], weff[:, i % 2, :, :]).then_inc(whi_done, 1)
                if i == 0:
                    high_t(0, 0)
                if i + 2 < NJ:
                    first_products(i + 2)
                if i == 2:
                    act.wait_ge(wt_ready, 1)
                    nc.scalar.mul(wqkvT[:, 0:C], work[:, 1, 0:C], SCALE).then_inc(wt_copied, 1)
                    nc.scalar.copy(wqkvT[:, C:3 * C], work[:, 1, C:3 * C]).then_inc(wt_copied, 1)
                    nc.scalar.copy(w2T[:, :], work[:, 0, 0:2 * C]).then_inc(wt_copied, 1)
                    nc.scalar.mul(bq_s[:, :], bqk[:, 0:1], SCALE).then_inc(consts_done, 1)
                if i == 3:
                    act.wait_ge(wt_copied, 3)
                    nc.scalar.copy(w2hi[:, :], w2T[:, :]).then_inc(small_hi_done, 1)
                    nc.scalar.copy(wqhi[:, :], wqkvT[:, :]).then_inc(small_hi_done, 1)
            act.wait_ge(b1_done, 1)

            def body(n, par, conv, attn, more):
                def exp(i):
                    if i % 2 == 0:
                        act.wait_ge(max_done, n * 4 + (i // 2 - 3))
                    nc.scalar.activation(p_sb[:, i, :], s_ps[:, (i // 2) % 2, (i % 2) * SC:(i % 2 + 1) * SC],
                                         ACT.Exp, bias=negmax[:, i:i + 1],
                                         accum_out=p_sum[:, i:i + 1]).then_inc(p_done, 1)

                def take_pt(g):
                    act.wait_ge(pt_ready, n * 2 + (g - 1))
                    tiles = slice(4 * g, 4 * g + 4)
                    main = work[:, 2 if g == 0 else 0, :]
                    rest = work[0:REST, 0, :] if g == 0 else s_ps[0:REST, 0, :]
                    nc.scalar.copy(pt_main[:, tiles, :], main.rearrange("p (t q) -> p t q", t=4)).then_inc(ptm_done, 1)
                    nc.scalar.copy(pt_rest[:, tiles, :], rest.rearrange("p (t q) -> p t q", t=4)).then_inc(ptr_done, 1)

                if attn:
                    gelu(n - 1, 1)
                if conv:
                    take_m13(n, 0)
                if more:
                    spread_x(n + 1, 1 - par)
                if isinstance(n, int) and n == 1:
                    act.wait_ge(consts_done, 1)
                if attn:
                    for c in range(NCH):
                        act.wait_ge(q_ready, n * 2 + (c - 1))
                        nc.scalar.activation(q_sb[:, c * CH:(c + 1) * CH], work[:, 2 if c == 0 else 0, :],
                                             ACT.Identity, bias=bq_s[:, :]).then_inc(q_done, 1)
                    for c in range(NCH):
                        act.wait_ge(k_ready, n * 2 + (c - 1))
                        nc.scalar.activation(k_sb[:, c * CH:(c + 1) * CH], work[:, 1 if c == 0 else 2, :],
                                             ACT.Identity, bias=bqk[:, 1:2]).then_inc(k_done, 1)
                if attn:
                    for i in range(4):
                        exp(i)
                if more:
                    high_t(n + 1, 1 - par)
                if conv:
                    take_m13(n, 1)
                if attn:
                    for i in range(4, T):
                        exp(i)
                    take_pt(0)
                if conv:
                    gelu(n, 0)
                if attn:
                    take_pt(1)

            steady(act, body)

        @block.vector
        def _(dve):
            dve.wait_ge(filters_in, 64)
            g0, g1, g2 = (wp[:, :, :, i] for i in range(3))
            done = [0]

            def step(instruction):
                done[0] += 1
                instruction.then_inc(filters_done, 1)

            step(nc.vector.tensor_tensor(gt[:, 0, :, :], g0, g2, ALU.add))
            step(nc.vector.tensor_scalar(gt[:, 1, :, :], g2, 1 / 6, None, ALU.mult))
            step(nc.vector.tensor_scalar(gt[:, 3, :, :], g1, 1 / 12, None, ALU.mult))
            step(nc.vector.tensor_scalar(wg[:, 0, :, :], g0, 1 / 4, None, ALU.mult))
            step(nc.vector.tensor_copy(wg[:, 5, :, :], g2))
            dve.wait_ge(filters_done, 2)
            step(nc.vector.scalar_tensor_tensor(out=gt[:, 2, :, :], in0=g0, scalar=1 / 24, in1=gt[:, 1, :, :],
                                                op0=ALU.mult, op1=ALU.add))
            step(nc.vector.tensor_tensor(wg[:, 1, :, :], gt[:, 0, :, :], g1, ALU.add))
            step(nc.vector.tensor_tensor(wg[:, 2, :, :], gt[:, 0, :, :], g1, ALU.subtract))
            dve.wait_ge(filters_done, 8)
            step(nc.vector.tensor_tensor(wg[:, 3, :, :], gt[:, 2, :, :], gt[:, 3, :, :], ALU.add))
            step(nc.vector.tensor_tensor(wg[:, 4, :, :], gt[:, 2, :, :], gt[:, 3, :, :], ALU.subtract))
            step(nc.vector.tensor_scalar(wg[:, 1:3, :, :], wg[:, 1:3, :, :], -1 / 6, None, ALU.mult))
            dve.wait_ge(w1t_ready, 1)
            for m in range(3):
                nc.vector.tensor_copy(w1T[:, m, :], m_ps[:, m, 0:HID]).then_inc(w1t_copied, 1)
            dve.wait_ge(w1t_copied, 3)
            dve.wait_ge(filters_done, 11)

            def rows(a):
                return a.rearrange("p (r w) -> p r w", w=WIN)

            def transform_ab(n, par):
                d1, d2, d3, d4 = (xp[:, par, k, :, 1:WIN + 1] for k in range(K4))
                dve.wait_ge(x_done, n + 1)
                if from_image(n, 1):
                    dve.wait_ge(tlo_done, n)
                nc.vector.scalar_tensor_tensor(out=rows(ab[:, 0, :]), in0=d2, scalar=-4.0, in1=d4, op0=ALU.mult,
                                               op1=ALU.add).then_inc(ab_done, 1)
                nc.vector.scalar_tensor_tensor(out=rows(ab[:, 1, :]), in0=d1, scalar=-4.0, in1=d3, op0=ALU.mult,
                                               op1=ALU.add).then_inc(ab_done, 1)

            def transform(n, par):
                dve.wait_ge(fcge_done, n * 3 + 3)
                f, c, g, e = fc[:, 0, :], fc[:, 1, :], ge[:, 0, :], ge[:, 1, :]
                for j, a, by, b in ((3, f, 2.0, c), (4, f, -2.0, c), (0, g, 4.0, c), (5, f, -4.0, e)):
                    nc.vector.scalar_tensor_tensor(out=t[:, j, :], in0=a, scalar=by, in1=b, op0=ALU.mult,
                                                   op1=ALU.add).then_inc(td_done, 1)

            for i, j in enumerate(M_ORDER):
                for m in (1, 2):
                    for dy in range(3):
                        if m == 1:
                            dve.wait_ge(weff0_done, 3 * i + dy + 1)
                        else:
                            dve.wait_ge(weff_done, 6 * i + dy + 1)
                        nc.vector.scalar_tensor_tensor(out=weff[:, i % 2, dy, :], in0=w1T[:, m, :],
                                                       scalar=wg[:, j, m, dy:dy + 1], in1=weff[:, i % 2, dy, :],
                                                       op0=ALU.mult, op1=ALU.add).then_inc(weff_done, 1)
                if i == 0:
                    transform_ab(0, 0)
                    transform(0, 0)
                if i == 4:
                    dve.wait_ge(b1_ready, 1)
                    nc.vector.tensor_tensor(b1eff[:, :], work[:, 2, 0:2], b1[:, :], ALU.add).then_inc(b1_done, 1)
                    dve.wait_ge(small_hi_done, 2)
                    nc.vector.tensor_tensor(w2lo[:, :], w2T[:, :], w2hi[:, :].bitcast(F32),
                                            ALU.subtract).then_inc(small_lo_done, 1)
                    nc.vector.tensor_tensor(wqlo[:, :], wqkvT[:, :], wqhi[:, :].bitcast(F32),
                                            ALU.subtract).then_inc(small_lo_done, 1)

            def combine(n, half):
                i = half + 1
                dve.wait_ge(m13_done, n * 2 + i)
                dve.wait_ge(m_ready, n * 6 + (3 * half + 2))
                if half or from_image(n, 1):
                    dve.wait_ge(y_part_done, n * 8 + 4 * half)
                nc.vector.tensor_tensor(ps_sb[:, :], m13[:, :], m_ps[:, 1, :], ALU.add).then_inc(ps_done, 1)
                nc.vector.tensor_tensor(ru_sb[:, :], m13[:, :], m_ps[:, 1, :], ALU.subtract).then_inc(ru_done, 1)

            def combine_y(n, half):
                i = half + 1
                if from_image(n, 1):
                    dve.wait_ge(hid_done, n * 2 + (half - 1))
                p, s, r, u = ps_sb[:, 0:S], ps_sb[:, S:CH], ru_sb[:, 0:S], ru_sb[:, S:CH]
                dve.wait_ge(ps_done, n * 2 + i)
                nc.vector.tensor_tensor(y[:, half, 0, :], p, s, ALU.add).then_inc(y_part_done, 1)
                nc.vector.scalar_tensor_tensor(out=y[:, half, 3, :], in0=s, scalar=4.0, in1=p, op0=ALU.mult,
                                               op1=ALU.add).then_inc(y_part_done, 1)
                dve.wait_ge(ru_done, n * 2 + i)
                nc.vector.scalar_tensor_tensor(out=y[:, half, 1, :], in0=u, scalar=8.0, in1=r, op0=ALU.mult,
                                               op1=ALU.add).then_inc(y_part_done, 1)
                nc.vector.scalar_tensor_tensor(out=y[:, half, 2, :], in0=u, scalar=2.0, in1=r, op0=ALU.mult,
                                               op1=ALU.add).then_inc(y_part_done, 1)

            def finish_y(n, half):
                dve.wait_ge(m_ready, n * 6 + (3 * half + 3))
                dve.wait_ge(y_part_done, n * 8 + (4 * half + 3))
                y03 = y[:, half, 0:2, :].rearrange("p k s -> p (k s)")
                nc.vector.tensor_tensor(y03, y03, m_ps[:, 2, :], ALU.add).then_inc(y_done, 1)

            def high_hid(n, half):
                dve.wait_ge(hid_done, n * 2 + (half + 1))
                nc.vector.tensor_copy(hid_hi[:, half, :], hid[:, half, :]).then_inc(hid_hi_done, 1)

            def row_max(n, j):
                dve.wait_ge(s_ready, n * 4 + (j - 3))
                nc.vector.tensor_reduce(negmax[:, 2 * j:2 * j + 2],
                                        s_ps[:, j % 2, 0:2 * SC].rearrange("p (a b) -> p a b", a=2), AX.X,
                                        ALU.max, negate=True).then_inc(max_done, 1)

            def finish(n, g):
                tiles = slice(4 * g, 4 * g + 4)
                dve.wait_ge(o_ready, n * 2 + (g - 1))
                if from_image(n, 2):
                    dve.wait_ge(stored[g], n * 16 - 16)
                nc.vector.tensor_tensor(out_sb[:, tiles, :],
                                        work[:, 2 if g == 0 else 0, :].rearrange("p (t c) -> p t c", t=4),
                                        rsum[:, tiles].unsqueeze(2).to_broadcast([P, 4, C]),
                                        ALU.mult).then_inc(om_done, 1)
                dve.wait_ge(om_done, n * 2 + (g - 1))
                dve.wait_ge(hp_ready, n * 2 + (g - 1))
                hp = work[:, 1, :] if g == 0 else s_ps[:, 1, :]
                nc.vector.tensor_tensor(out_sb[:, tiles, :], out_sb[:, tiles, :],
                                        hp.rearrange("p (t c) -> p t c", t=4), ALU.add).then_inc(out_done, 1)

            def body(n, par, conv, attn, more):
                if attn:
                    high_hid(n - 1, 1)
                    by_plane = h.rearrange("p (r w k) -> p k r w", k=K4, w=WIN)
                    for i, k in enumerate(PLANES):
                        if i % 2 == 0:
                            dve.wait_ge(up_ready, n * 2 + (i // 2 - 1))
                        nc.vector.scalar_tensor_tensor(
                            out=by_plane[:, k, :, :],
                            in0=work[:, i // 2, (i % 2) * S:(i % 2 + 1) * S].rearrange("p (r w) -> p r w", w=WIN),
                            scalar=b2[:, 0:1], in1=xp[:, 1 - par, k, 1:H + 1, 1:WIN + 1], op0=ALU.add,
                            op1=ALU.add).then_inc(h_done, 1)
                    dve.wait_ge(h_done, n * 4)
                    for c in range(NCH):
                        cols = slice(c * CH, (c + 1) * CH)
                        nc.vector.tensor_copy(h_hi[:, cols], h[:, cols]).then_inc(h_hi_done, 1)
                    for c in range(NCH):
                        cols = slice(c * CH, (c + 1) * CH)
                        dve.wait_ge(h_hi_done, n * 2 + (c - 1))
                        nc.vector.tensor_tensor(h_lo[:, cols], h[:, cols], h_hi[:, cols].bitcast(F32),
                                                ALU.subtract).then_inc(h_lo_done, 1)
                if conv:
                    combine(n, 0)
                if conv:
                    combine_y(n, 0)
                    finish_y(n, 0)
                if attn:
                    for g in range(2):
                        dve.wait_ge(v_ready, n * 3 + (g - 2))
                        nc.vector.tensor_tensor(v_sb[:, 4 * g:4 * g + 4, :],
                                                work[:, g, :].rearrange("p (t c) -> p t c", t=4),
                                                bv[:, :].unsqueeze(1).to_broadcast([P, 4, C]),
                                                ALU.add).then_inc(v_done, 1)
                    dve.wait_ge(v_ready, n * 3)
                    nc.vector.tensor_tensor(v_sb[0:REST, T, :], work[0:REST, 2, 0:C], bv[0:REST, :],
                                            ALU.add).then_inc(v_done, 1)
                if more:
                    transform_ab(n + 1, 1 - par)
                if attn:
                    row_max(n, 0)
                    row_max(n, 1)
                if more:
                    transform(n + 1, 1 - par)
                if attn:
                    row_max(n, 2)
                    row_max(n, 3)
                if conv:
                    combine(n, 1)
                    combine_y(n, 1)
                if attn:
                    dve.wait_ge(p_done, n * 8)
                    nc.vector.reciprocal(rsum[:, :], p_sum[:, :]).then_inc(rsum_done, 1)
                    dve.wait_ge(rsum_done, n)
                    finish(n, 0)
                if conv:
                    high_hid(n, 0)
                    finish_y(n, 1)
                if attn:
                    finish(n, 1)

            steady(dve, body)

        @block.gpsimd
        def _(pool):
            nc.gpsimd.memset(xp[:, :, :, :, :], 0.0).then_inc(zeroed, 1)
            nc.gpsimd.memset(h_around[:, 0:W], 0.0).then_inc(zeroed, 1)
            nc.gpsimd.memset(h_around[:, W + PIX:], 0.0).then_inc(zeroed, 1)

            def differences(n, par):
                def plane(k, shift=0):
                    return xp[:, par, k, :, 1 + shift:WIN + 1 + shift]

                def rows(a):
                    return a.rearrange("p (r w) -> p r w", w=WIN)

                pool.wait_ge(x_done, n + 1)
                if from_image(n, 1):
                    pool.wait_ge(td_done, n * 4)
                nc.gpsimd.tensor_tensor(fc[:, :, :].rearrange("p a (r w) -> p a r w", w=WIN),
                                        xp[:, par, 2:4, :, 1:WIN + 1], xp[:, par, 0:2, :, 1:WIN + 1],
                                        ALU.subtract).then_inc(fcge_done, 1)
                nc.gpsimd.tensor_tensor(rows(ge[:, 0, :]), plane(3, -1), plane(1), ALU.subtract).then_inc(fcge_done, 1)
                nc.gpsimd.tensor_tensor(rows(ge[:, 1, :]), plane(0, 1), plane(2), ALU.subtract).then_inc(fcge_done, 1)
                pool.wait_ge(ab_done, n * 2 + 2)
                nc.gpsimd.tensor_tensor(t[:, 1, :], ab[:, 0, :], ab[:, 1, :], ALU.add).then_inc(tp_done, 1)
                nc.gpsimd.tensor_tensor(t[:, 2, :], ab[:, 0, :], ab[:, 1, :], ALU.subtract).then_inc(tp_done, 1)

            def low_t(n, par):
                pool.wait_ge(thi_done, n + 1)
                nc.gpsimd.tensor_tensor(tlo[:, par, :, :], t[:, :, :], thi[:, par, :, :].bitcast(F32),
                                        ALU.subtract).then_inc(tlo_done, 1)

            def low_hid(n, half):
                pool.wait_ge(hid_hi_done, n * 2 + (half + 1))
                for c in range(NCH):
                    cols = slice(c * CH, (c + 1) * CH)
                    nc.gpsimd.tensor_tensor(hid_lo[:, half, cols], hid[:, half, cols],
                                            hid_hi[:, half, cols].bitcast(F32), ALU.subtract).then_inc(hid_lo_done, 1)

            differences(0, 0)
            for i, j in enumerate(M_ORDER):
                pool.wait_ge(whi_done, i + 1)
                nc.gpsimd.tensor_tensor(wlo[:, j, :, :], weff[:, i % 2, :, :], whi[:, j, :, :].bitcast(F32),
                                        ALU.subtract).then_inc(wlo_done, 1)
                if i == 0:
                    low_t(0, 0)

            def body(n, par, conv, attn, more):
                if attn:
                    low_hid(n - 1, 1)
                if more:
                    differences(n + 1, 1 - par)
                    low_t(n + 1, 1 - par)
                if conv:
                    low_hid(n, 0)

            steady(pool, body)


_INS = ["x", "L0_conv_w_perc", "L0_conv_b_perc", "L0_conv_w_up1", "L0_conv_b_up1", "L0_conv_w_up2",
        "L0_conv_b_up2", "L0_conv_w_qkv", "L0_conv_b_qkv"]


def kernel(**inputs):
    import concourse.bacc as bacc
    import ml_dtypes
    from concourse.bass_utils import run_bass_kernel_spmd as run

    nc = bacc.Bacc("TRN2", target_bir_lowering=False, num_devices=1)
    arrays = {name: np.ascontiguousarray(inputs[name]) for name in _INS}
    arrays["identity"] = np.eye(P, dtype=np.float32)
    arrays["identity_bf16"] = np.eye(P, dtype=ml_dtypes.bfloat16)
    arrays["masks"] = window_masks(ml_dtypes.bfloat16)
    args = [nc.dram_tensor(name, a.shape, mybir.dt.from_np(a.dtype), kind="ExternalInput").ap()
            for name, a in arrays.items()]
    out = nc.dram_tensor("out", (B, H, W, C), F32, kind="ExternalOutput").ap()
    build(nc, *args, out)
    r = run(nc, [arrays], core_ids=[0])
    return r.results[0]["out"]
```

```python
from contextlib import ExitStack

import numpy as np

import concourse.bass as bass
from concourse import mybir
from concourse.alu_op_type import AluOpType as ALU

ACT = mybir.ActivationFunctionType
AX = mybir.AxisListType
F32 = mybir.dt.float32
F32R = mybir.dt.float32r
BF16 = mybir.dt.bfloat16

P = 128
B, H, W, C = 16, 32, 32, 128
PIX = H * W
TR = P // W
T = H // TR
CH = 512
NCH = PIX // CH
HID = 2 * C
WINDOW = P + 2 * W
VT = C + 1
NEG = -1e30
SCALE = float(C) ** -0.5

K4 = 4
WIN = W // K4
S = H * WIN
NJ = 6
TS = (H + 2) * WIN
PLANES = (0, 3, 1, 2)
M_PLACE = {1: (0, 0), 3: (0, S), 2: (1, 0), 4: (1, S), 0: (2, 0), 5: (2, S)}
M_ORDER = (1, 3, 2, 4, 0, 5)
T_PLACE = {j: i for i, j in enumerate(M_ORDER)}
T_PARTS = (slice(0, 4), slice(4, 6))


def window_masks(dtype):
    m = np.full((P, 4, WINDOW), NEG, dtype)
    for kind in range(4):
        for qy in range(TR):
            for qx in range(W):
                for ky in range(-1, TR + 1):
                    if abs(ky - qy) > 1 or (kind == 0 and ky < 0) or (kind == 3 and ky >= TR):
                        continue
                    for kx in range(max(0, qx - 1), min(W, qx + 2)):
                        m[qy * W + qx, kind, (ky + 1) * W + kx] = 0.0
    return m


def zero_keys():
    z = np.zeros((P, 2, T), np.float32)
    for i in range(T):
        for q in range(P):
            qy, qx = i * TR + q // W, q % W
            rows = 3 - (qy == 0) - (qy == H - 1)
            cols = 3 - (qx == 0) - (qx == W - 1)
            z[q, 0, i] = 9 - rows * cols
            z[q, 1, i] = 0.0 if rows * cols < 9 else -NEG
    return z


def build(nc, x, w_perc, b_perc, w_up1, b_up1, w_up2, b_up2, w_qkv, b_qkv, ident_c, ident_bf_c, mask_c, zero_c, out):
    with ExitStack() as ctx:
        def sb(name, shape, dt=F32):
            return ctx.enter_context(nc.sbuf_tensor(name, shape, dt))

        def sem(name):
            return ctx.enter_context(nc.semaphore(name))

        def psum(name, banks):
            return ctx.enter_context(nc.psum_tensor(name, [P, banks, CH], F32))

        m_ps = psum("m_ps", 3)
        s_ps = psum("s_ps", 2)
        work = psum("work", 3)

        ident = sb("ident", [P, P])
        ident_bf = sb("ident_bf", [P, P], BF16)
        mask_bf = sb("mask_bf", [P, 4, WINDOW], BF16)
        wp = sb("wp", [P, 3, 3, 3])
        bp = sb("bp", [P, 3])
        b1 = sb("b1", [P, 2])
        b2 = sb("b2", [P, 1])
        bqk = sb("bqk", [P, 2])
        bv = sb("bv", [P, C])
        w1T = sb("w1T", [P, 3, HID])
        w2T = sb("w2T", [P, 2 * C])
        w2hi = sb("w2hi", [P, 2 * C], F32R)
        w2lo = sb("w2lo", [P, 2 * C], F32R)
        wvT = sb("wvT", [P, VT])
        wqk = sb("wqk", [P, C])
        wqk_hi = sb("wqk_hi", [P, C], F32R)
        wqk_lo = sb("wqk_lo", [P, C], F32R)
        bq_wide = sb("bq_wide", [P, P])
        zeros = sb("zeros", [P, 2, T])
        bqk_s = sb("bqk_s", [P, 1])
        z_base = sb("z_base", [P, T])
        b1eff = sb("b1eff", [P, 2])
        bq_s = sb("bq_s", [P, 1])
        wg = sb("wg", [P, NJ, 3, 3])
        gt = sb("gt", [P, 4, 3, 3])
        primer = sb("primer", [P, 1])
        whi = sb("whi", [P, NJ, 3, HID], F32R)
        wlo = sb("wlo", [P, NJ, 3, HID], F32R)

        x_in = sb("x_in", [P, 2, 2, K4, C])
        xp = sb("xp", [P, 2, K4, H + 2, WIN + 2])
        xr = sb("xr", [P, K4, S])
        fc = sb("fc", [P, 2, TS])
        ge = sb("ge", [P, 2, TS])
        ab = sb("ab", [P, 2, TS])
        t = sb("t", [P, NJ, TS])
        thi = sb("thi", [P, 2, NJ, TS], F32R)
        tlo = sb("tlo", [P, 2, NJ, TS], F32R)
        m13 = sb("m13", [P, CH])
        ps_sb = sb("ps_sb", [P, CH])
        ru_sb = sb("ru_sb", [P, CH])
        y = sb("y", [P, 2, K4, S])
        hid = sb("hid", [P, 2, PIX])
        hid_hi = sb("hid_hi", [P, 2, PIX], F32R)
        hid_lo = sb("hid_lo", [P, 2, PIX], F32R)
        h_around = sb("h_around", [P, W + PIX + W])
        h = h_around[:, W:W + PIX]
        h_hi = sb("h_hi", [P, PIX], F32R)
        h_lo = sb("h_lo", [P, PIX], F32R)
        q_sb = sb("q_sb", [P, PIX])
        v_sb = sb("v_sb", [P, T, C])
        nz = sb("nz", [P, T])
        negmax = sb("negmax", [P, T])
        z_arg = sb("z_arg", [P, T])
        z_exp = sb("z_exp", [P, T])
        p_sum = sb("p_sum", [P, T])
        rsum = sb("rsum", [P, T])
        p_sb = sb("p_sb", [P, T, WINDOW])
        pt = sb("pt", [P, T, WINDOW])
        o_sb = sb("o_sb", [P, PIX])
        out_sb = sb("out_sb", [P, T, C])

        w1 = y[:, :, :, :].rearrange("p h k s -> p h (k s)")[:, :, 0:3 * C]
        wqkv = h[:, 0:3 * C].rearrange("p (j c) -> p j c", j=3)
        w2 = h[:, 3 * C:3 * C + HID]

        p_flat, v_flat, out_flat = (a[:, :, :].rearrange("p t c -> p (t c)") for a in (p_sb, v_sb, out_sb))
        weff = [a.rearrange("p (d o) -> p d o", d=3) for a in
                (p_flat[:, 0:3 * HID], p_flat[:, 3 * HID:6 * HID], o_sb[:, 0:3 * HID], out_flat[:, 0:3 * HID],
                 v_flat[:, 0:3 * HID], q_sb[:, 0:3 * HID])]

        first_in = sem("first_in")
        filters_in = sem("filters_in")
        biases_in = sem("biases_in")
        weights_in = sem("weights_in")
        x_loaded = [sem(f"x_loaded{i}") for i in range(2)]
        stored = [sem(f"stored{i}") for i in range(2)]
        zeroed = sem("zeroed")
        w1t_ready = sem("w1t_ready")
        wt_ready = sem("wt_ready")
        w1t_copied = sem("w1t_copied")
        wt_copied = sem("wt_copied")
        b1_ready = sem("b1_ready")
        b1_done = sem("b1_done")
        z_base_done = sem("z_base_done")
        filters_done = sem("filters_done")
        weff0_done = sem("weff0_done")
        weff_done = sem("weff_done")
        whi_done = sem("whi_done")
        wlo_ends_done = sem("wlo_ends_done")
        wlo_done = sem("wlo_done")
        primed = sem("primed")
        bq_wide_done = sem("bq_wide_done")
        consts_done = sem("consts_done")
        small_hi_done = sem("small_hi_done")
        small_lo_done = sem("small_lo_done")
        xt_ready = sem("xt_ready")
        m_ready = sem("m_ready")
        up_ready = sem("up_ready")
        q_ready = sem("q_ready")
        v_ready = sem("v_ready")
        s_ready = sem("s_ready")
        pt_ready = sem("pt_ready")
        o_ready = sem("o_ready")
        ot_ready = sem("ot_ready")
        x_done = sem("x_done")
        thi_done = sem("thi_done")
        xr_done = sem("xr_done")
        m13_done = sem("m13_done")
        hid_done = sem("hid_done")
        q_done = sem("q_done")
        z_exp_done = sem("z_exp_done")
        p_done = sem("p_done")
        pt_done = sem("pt_done")
        out_done = sem("out_done")
        ab_done = sem("ab_done")
        td_done = sem("td_done")
        ps_done = sem("ps_done")
        ru_done = sem("ru_done")
        y_part_done = sem("y_part_done")
        y_done = sem("y_done")
        hid_hi_done = sem("hid_hi_done")
        h_done = sem("h_done")
        h_hi_done = sem("h_hi_done")
        h_lo_done = sem("h_lo_done")
        v_done = sem("v_done")
        max_done = sem("max_done")
        rmax_done = sem("rmax_done")
        z_arg_done = sem("z_arg_done")
        sums_done = sem("sums_done")
        rsum_done = sem("rsum_done")
        edges_done = sem("edges_done")
        hid_lo_last_done = sem("hid_lo_last_done")
        pn_last_done = sem("pn_last_done")
        o_done = sem("o_done")
        fcge_done = sem("fcge_done")
        tp_done = sem("tp_done")
        tlo_done = sem("tlo_done")
        pn_done = sem("pn_done")
        hid_lo_done = sem("hid_lo_done")

        x_dram = x.rearrange("b (g r) (w k) c -> b (r w) g k c", g=2, k=K4)
        out_dram = out.rearrange("b (t r) w c -> b (r w) t c", r=TR)
        V_PARTS = (range(0, 3), range(3, 6), range(6, 8))
        N_W = 7

        def steady(eng, body, last=None):
            body(0, 0, True, False, False, True)
            body(1, 1, True, True, False, True)
            body(2, 0, True, True, True, True)
            body(3, 1, True, True, True, True)
            with eng.Fori(0, (B - 6) // 2) as m:
                body(m * 2 + 4, 0, True, True, True, True)
                body(m * 2 + 5, 1, True, True, True, True)
            body(B - 2, 0, True, True, True, True)
            body(B - 1, 1, True, True, True, False)
            body(B, 0, False, True, True, False)
            if last:
                last(B + 1)

        def is_last(n):
            return isinstance(n, int) and n == B

        def up_bank(n, c):
            return m_ps[:, c, :] if is_last(n) else work[:, c, :]

        def v_bank(n, part):
            if is_last(n):
                return (work[:, 1, :], m_ps[:, 0, :], m_ps[:, 1, :])[part]
            return work[:, (1, 2, 0)[part], :]

        def s_bank(n, j):
            if is_last(n):
                return (s_ps[:, 0, :], s_ps[:, 1, :], m_ps[:, 2, :], m_ps[:, 0, :])[j]
            return s_ps[:, j % 2, :]

        def from_image(n, base):
            return not isinstance(n, int) or n >= base

        block = ctx.enter_context(nc.Block())

        @block.sync
        def _(sp):
            def load(dst, src, **kw):
                sp.dma_start(dst, src, **kw).then_inc(weights_in, 16)

            sp.dma_start(ident[:, :], ident_c).then_inc(first_in, 16)
            sp.dma_start(w1, w_up1.rearrange("(h p) k a b -> p h (k a b)", p=P)).then_inc(first_in, 16)
            sp.dma_start(x_in[:, 0, :, :, :], x_dram[0]).then_inc(x_loaded[0], 16)
            load(w2, w_up2.rearrange("c k a b -> c (k a b)"))
            load(wqkv, w_qkv.rearrange("(j p) c -> p j c", p=P))
            load(bqk[:, :], b_qkv[0:2 * C].rearrange("(j p) -> p j", p=P), allow_slow_non_contiguous=True)
            load(bv[:, :], b_qkv[2 * C:3 * C].partition_broadcast(P))
            load(mask_bf[:, :, :], mask_c)
            load(ident_bf[:, :], ident_bf_c)
            load(zeros[:, :, :], zero_c)
            sp.dma_start(x_in[:, 1, :, :, :], x_dram[1]).then_inc(x_loaded[1], 16)

            def store_out(n):
                for g in range(2):
                    sp.wait_ge(out_done, n * 2 - 3 + g)
                    sp.dma_start(out_dram[n - 2][:, g * 4:g * 4 + 4, :],
                                 out_sb[:, g * 4:g * 4 + 4, :]).then_inc(stored[g], 16)

            def body(n, par, conv, attn, store, more):
                if conv and (not isinstance(n, int) or n + 2 < B):
                    sp.wait_ge(xt_ready, n + 1)
                    sp.dma_start(x_in[:, par, :, :, :], x_dram[n + 2]).then_inc(x_loaded[par], 16)
                if store:
                    store_out(n)

            steady(sp, body, last=store_out)
            for g in range(2):
                sp.wait_ge(stored[g], 16 * B)

        @block.tensor
        def _(pe):
            pe.wait_ge(first_in, 32)
            for m in range(3):
                for g in range(2):
                    last = pe.transpose(m_ps[:, m, g * P:(g + 1) * P], w1[:, g, m:3 * C:3], ident[:, :])
            last.then_inc(w1t_ready, 1)

            def small_weights():
                pe.wait_ge(weights_in, 16 * N_W)
                for g in range(2):
                    pe.transpose(work[:, 0, g * P:(g + 1) * P], w2[:, g * P:(g + 1) * P], ident[:, :])
                pe.transpose(work[:, 1, 0:P], wqkv[:, 2, :], ident[:, :])
                wq, wk = wqkv[:, 0, :], wqkv[:, 1, :]
                pe.matmul(work[:, 1, P:2 * P], wq, wk, start=True, stop=True)
                pe.matmul(work[:, 1, 2 * P:2 * P + 1], wq, bqk[:, 1:2], start=True, stop=True)
                pe.matmul(work[:, 1, 2 * P + 1:2 * P + 2], wk, bqk[:, 0:1], start=True, stop=True)
                pe.wait_ge(bq_wide_done, 1)
                pe.matmul(work[:, 1, 2 * P + 2:2 * P + 3], bq_wide[:, :], bqk[:, 1:2], start=True,
                          stop=True).then_inc(wt_ready, 1)
                pe.wait_ge(biases_in, 48)
                pe.wait_ge(w1t_copied, 3)
                for g in range(2):
                    for m in range(3):
                        last = pe.matmul(work[:, 2, g:g + 1], w1T[:, m, g * P:(g + 1) * P], bp[:, m:m + 1],
                                         start=(m == 0), stop=(m == 2))
                last.then_inc(b1_ready, 1)

            def transpose_x(n, par):
                pe.wait_ge(x_loaded[par], n * 8 + (8 if par else 16))
                for k in range(K4):
                    for g in range(2):
                        i = 2 * k + g
                        last = pe.transpose(s_ps[:, i // 4, (i % 4) * P:(i % 4 + 1) * P], x_in[:, par, g, k, :],
                                            ident[:, :])
                last.then_inc(xt_ready, 1)

            def unit(n, par, i):
                half, i = divmod(i, NJ)
                j = M_ORDER[i]
                b, col = M_PLACE[j]
                if half == 0 and i in (0, 4):
                    pe.wait_ge(thi_done, n * 2 + (1 if i == 0 else 2))
                    pe.wait_ge(tlo_done, n * 2 + (1 if i == 0 else 2))
                if col == 0 and (half == 1 or from_image(n, 1)):
                    pe.wait_ge((m13_done, ru_done, y_done)[b], n * 2 + half)
                if isinstance(n, int) and n == 0 and half == 0:
                    if i in (0, NJ - 1):
                        pe.wait_ge(wlo_ends_done, 1 if i == 0 else 2)
                    else:
                        pe.wait_ge(wlo_done, i)
                steps = [(dy, a, c) for dy in range(3) for a, c in ((whi, thi), (whi, tlo), (wlo, thi))]
                for s, (dy, a, c) in enumerate(steps):
                    last = pe.matmul(m_ps[:, b, col:col + S], a[:, j, dy, half * P:(half + 1) * P],
                                     c[:, par, T_PLACE[j], dy * WIN:dy * WIN + S], start=(s == 0),
                                     stop=(s == len(steps) - 1))
                if col:
                    last.then_inc(m_ready, 1)

            def up(n, c):
                if is_last(n):
                    pe.wait_ge(hid_lo_last_done, c + 1)
                else:
                    pe.wait_ge(hid_lo_done, n * 4 + (c - 1))
                i = 0
                for half in range(2):
                    for a, b in ((w2hi, hid_hi), (w2hi, hid_lo), (w2lo, hid_hi)):
                        last = pe.matmul(up_bank(n, c), a[:, half * C:(half + 1) * C],
                                         b[:, half, c * CH:(c + 1) * CH], start=(i == 0), stop=(i == 5))
                        i += 1
                last.then_inc(up_ready, 1)

            def project_q(c, b):
                cols = slice(c * CH, (c + 1) * CH)
                pe.matmul(work[:, b, :], wqk_hi[:, :], h_hi[:, cols], start=True, stop=False)
                pe.matmul(work[:, b, :], wqk_hi[:, :], h_lo[:, cols], start=False, stop=False)
                pe.matmul(work[:, b, :], wqk_lo[:, :], h_hi[:, cols], start=False, stop=True).then_inc(q_ready, 1)

            def project_v(n, part):
                for u, i in enumerate(V_PARTS[part]):
                    last = pe.matmul(v_bank(n, part)[:, u * VT:(u + 1) * VT], h[:, i * P:(i + 1) * P], wvT[:, :],
                                     start=True, stop=True)
                last.then_inc(v_ready, 1)

            def scores(n, j):
                if is_last(n):
                    if j == 3:
                        pe.wait_ge(v_done, n * 6 - 2)
                elif j >= 2:
                    pe.wait_ge(p_done, n * 8 + (2 * j - 10))
                s = s_bank(n, j)
                kinds = 0 if j == 0 else 2 if j == T // 2 - 1 else 1
                pe.matmul(s[:, 0:2 * WINDOW], ident_bf[:, :],
                          mask_bf[:, kinds:kinds + 2, :].rearrange("p a b -> p (a b)"), start=True, stop=False,
                          skip_group_check=True)
                for u in range(2):
                    i = 2 * j + u
                    last = pe.matmul(s[:, u * WINDOW:(u + 1) * WINDOW], q_sb[:, i * P:(i + 1) * P],
                                     h_around[:, i * P:i * P + WINDOW], start=False, stop=(u == 1),
                                     skip_group_check=True)
                last.then_inc(s_ready, 1)

            def transpose_p(n, g):
                if is_last(n) and g == 1:
                    pe.wait_ge(pn_last_done, 1)
                else:
                    pe.wait_ge(pn_done, n * 2 + (g - 1))
                pe.wait_ge(v_done, n * 6 + (2 * g - 4))
                for u in range(4):
                    last = pe.transpose(work[:, 1 + g, u * P:(u + 1) * P], p_sb[:, 4 * g + u, W:W + P], ident[:, :])
                last.then_inc(pt_ready, 1)

            def values(n, g):
                pe.wait_ge(v_done, n * 6 - 6)
                pe.wait_ge(pt_done, n * 2 + (g - 3))
                pe.wait_ge(edges_done, n * 4 + (2 * g - 6))
                half = T // 2 * TR
                blocks = [(i, max(i * TR - 1, g * half), min((i + 1) * TR + 1, (g + 1) * half)) for i in range(T)]
                blocks = [(i, first, end) for i, first, end in blocks if first < end]
                for i, first, end in blocks:
                    above = i * TR - 1
                    last = pe.matmul(work[:, g, (first - g * half) * W:(end - g * half) * W], v_sb[:, i, :],
                                     pt[:, i, (first - above) * W:(end - above) * W], start=(i == blocks[0][0]),
                                     stop=(i == blocks[-1][0]), skip_group_check=True)
                last.then_inc(o_ready, 1)

            def transpose_out(n, g):
                pe.wait_ge(o_done, n * 2 + (g - 3))
                for u in range(4):
                    last = pe.transpose(s_ps[:, g, u * P:(u + 1) * P], o_sb[:, (4 * g + u) * P:(4 * g + u + 1) * P],
                                        ident[:, :])
                last.then_inc(ot_ready, 1)

            def last_attention(n):
                pe.wait_ge(h_done, n * 2)
                project_v(n, 0)
                project_v(n, 1)
                pe.wait_ge(h_lo_done, n * 2 - 1)
                project_q(0, 2)
                pe.wait_ge(h_lo_done, n * 2)
                project_q(1, 0)
                project_v(n, 2)
                pe.wait_ge(out_done, n * 2 - 2)
                pe.wait_ge(q_done, n * 2 - 1)
                scores(n, 0)
                scores(n, 1)
                pe.wait_ge(q_done, n * 2)
                scores(n, 2)
                scores(n, 3)
                transpose_p(n, 0)
                values(n + 1, 0)
                transpose_p(n, 1)
                transpose_out(n + 1, 0)
                values(n + 1, 1)
                transpose_out(n + 1, 1)

            def body(n, par, conv, attn, store, more):
                def units(*which):
                    if conv:
                        for i in which:
                            unit(n, par, i)

                if isinstance(n, int) and n == 0:
                    transpose_x(0, 0)
                    small_weights()
                units(0)
                if store:
                    transpose_p(n - 1, 1)
                    values(n, 0)
                units(1)
                if not attn and conv:
                    transpose_x(n + 1, 1 - par)
                if store:
                    values(n, 1)
                units(2)
                if store and not is_last(n):
                    if more:
                        pe.wait_ge(x_done, n + 2)
                    transpose_out(n, 0)
                units(3)
                if store and not is_last(n):
                    transpose_out(n, 1)
                if isinstance(n, int) and n == 1:
                    pe.wait_ge(small_lo_done, 2)
                    pe.wait_ge(zeroed, 4)
                if is_last(n):
                    pe.wait_ge(y_done, n * 2)
                if attn:
                    up(n, 0)
                    up(n, 1)
                if is_last(n):
                    transpose_out(n, 0)
                    transpose_out(n, 1)
                units(4, 5)
                if is_last(n):
                    last_attention(n)
                    return
                if attn:
                    pe.wait_ge(h_done, n * 2)
                    project_v(n, 0)
                    pe.wait_ge(h_lo_done, n * 2 - 1)
                    project_q(0, 2)
                    pe.wait_ge(h_lo_done, n * 2)
                    project_q(1, 0)
                units(6)
                if attn:
                    pe.wait_ge(q_done, n * 2 - 1)
                    project_v(n, 1)
                    pe.wait_ge(q_done, n * 2)
                    project_v(n, 2)
                    if store:
                        pe.wait_ge(out_done, n * 2 - 2)
                    else:
                        pe.wait_ge(x_done, n + 2)
                    scores(n, 0)
                    scores(n, 1)
                units(7)
                if attn:
                    scores(n, 2)
                units(8)
                if attn:
                    scores(n, 3)
                units(9, 10, 11)
                if attn:
                    transpose_p(n, 0)
                if not isinstance(n, int) or n + 2 < B:
                    if attn:
                        pe.wait_ge(p_done, n * 8)
                    else:
                        pe.wait_ge(x_done, n + 2)
                    transpose_x(n + 2, par)

            steady(pe, body)

        @block.scalar
        def _(act):
            act.dma_start(wp[:, :, :, :], w_perc.rearrange("(c m) a y x -> c m (a y) x", m=3)).then_inc(filters_in, 16)
            act.dma_start(bp[:, :], b_perc.rearrange("(c m) -> c m", m=3)).then_inc(biases_in, 16)
            act.dma_start(b1[:, :], b_up1.rearrange("(h p) -> p h", p=P),
                          allow_slow_non_contiguous=True).then_inc(biases_in, 16)
            act.dma_start(b2[:, :], b_up2.rearrange("(p a) -> p a", a=1)).then_inc(biases_in, 16)

            def spread_x(n, par):
                act.wait_ge(xt_ready, n + 1)
                if from_image(n, 2):
                    act.wait_ge(xr_done, n * 2 - 2)
                nc.scalar.copy(xp[:, par, :, 1:H + 1, 1:WIN + 1],
                               s_ps[:, :, :].rearrange("p a (b r w) -> p (a b) r w", b=2, w=WIN)).then_inc(x_done, 1)

            def high_t(n, par):
                act.wait_ge(td_done, n * 4 + 4)
                act.wait_ge(tp_done, n * 2 + 2)
                for part in T_PARTS:
                    nc.scalar.copy(thi[:, par, part, :], t[:, part, :]).then_inc(thi_done, 1)

            def copy_x(n, par):
                if from_image(n, 1):
                    act.wait_ge(h_done, n * 2)
                for i, step in enumerate((3, 1)):
                    k = PLANES[2 * i]
                    planes = slice(k, k + step + 1, step)
                    nc.scalar.copy(xr[:, 2 * i:2 * i + 2, :].rearrange("p k (r w) -> p k r w", w=WIN),
                                   xp[:, par, planes, 1:H + 1, 1:WIN + 1]).then_inc(xr_done, 1)

            def take_m13(n, half):
                act.wait_ge(m_ready, n * 6 + (3 * half + 1))
                if half or from_image(n, 1):
                    act.wait_ge(ru_done, n * 2 + half)
                nc.scalar.copy(m13[:, :], m_ps[:, 0, :]).then_inc(m13_done, 1)

            def gelu(n, half):
                act.wait_ge(y_part_done, n * 8 + (4 * half + 4))
                act.wait_ge(y_done, n * 2 + (half + 1))
                if isinstance(n, int) and n == 0:
                    act.wait_ge(b1_done, 1)
                if from_image(n, 1):
                    act.wait_ge(hid_lo_done, n * 4 + (2 * half - 2))
                nc.scalar.activation(hid[:, half, :], y[:, half, :, :].rearrange("p k s -> p (k s)"), ACT.Gelu,
                                     bias=b1eff[:, half:half + 1]).then_inc(hid_done, 1)

            def first_products(i):
                for dy in range(3):
                    nc.scalar.activation(weff[i][:, dy, :], w1T[:, 0, :], ACT.Copy,
                                         scale=wg[:, M_ORDER[i], 0, dy:dy + 1]).then_inc(weff0_done, 1)

            def prime_gelu():
                nc.scalar.activation(primer[:, :], ident[:, 0:1], ACT.Gelu).then_inc(primed, 1)

            act.wait_ge(first_in, 32)
            prime_gelu()
            act.wait_ge(w1t_ready, 1)
            for m in range(3):
                nc.scalar.copy(w1T[:, m, :], m_ps[:, m, 0:HID]).then_inc(w1t_copied, 1)
            act.wait_ge(zeroed, 1)
            spread_x(0, 0)
            act.wait_ge(w1t_copied, 3)
            act.wait_ge(filters_done, 11)
            first_products(1)
            for i, j in enumerate(M_ORDER):
                act.wait_ge(weff_done, 6 * (i + 1) + 3)
                nc.scalar.copy(whi[:, j, :, :], weff[i]).then_inc(whi_done, 1)
                if i + 2 < NJ:
                    first_products(i + 2)
                if i == 0:
                    high_t(0, 0)
                if i == 3:
                    act.wait_ge(wt_ready, 1)
                    wa = work[:, 1, :]
                    nc.scalar.copy(wvT[:, 0:C], wa[:, 0:C]).then_inc(wt_copied, 1)
                    nc.scalar.mul(wqk[:, :], wa[:, C:2 * C], SCALE).then_inc(wt_copied, 1)
                    nc.scalar.mul(wvT[:, C:VT], wa[:, 2 * C:2 * C + 1], SCALE).then_inc(wt_copied, 1)
                    nc.scalar.copy(w2T[:, :], work[:, 0, 0:2 * C]).then_inc(wt_copied, 1)
                    nc.scalar.mul(bq_s[:, :], wa[:, 2 * C + 1:2 * C + 2], SCALE).then_inc(consts_done, 1)
                    nc.scalar.mul(bqk_s[:, :], wa[:, 2 * C + 2:2 * C + 3], SCALE).then_inc(consts_done, 1)
                if i == 4:
                    act.wait_ge(wt_copied, 4)
                    nc.scalar.copy(w2hi[:, :], w2T[:, :]).then_inc(small_hi_done, 1)
                    nc.scalar.copy(wqk_hi[:, :], wqk[:, :]).then_inc(small_hi_done, 1)
            def take_pt(n, g):
                act.wait_ge(pt_ready, n * 2 + (g - 1))
                nc.scalar.copy(pt[:, 4 * g:4 * g + 4, W:W + P],
                               work[:, 1 + g, :].rearrange("p (t q) -> p t q", t=4)).then_inc(pt_done, 1)

            def take_out(n, g):
                act.wait_ge(ot_ready, n * 2 + (g - 3))
                if from_image(n, 3):
                    act.wait_ge(stored[g], n * 16 - 32)
                nc.scalar.copy(out_sb[:, 4 * g:4 * g + 4, :],
                               s_ps[:, g, :].rearrange("p (t c) -> p t c", t=4)).then_inc(out_done, 1)

            def body(n, par, conv, attn, store, more):
                def exp(i):
                    if i % 2 == 0:
                        act.wait_ge(max_done, n * 4 + (i // 2 - 3))
                    nc.scalar.activation(p_sb[:, i, :], s_bank(n, i // 2)[:, (i % 2) * WINDOW:(i % 2 + 1) * WINDOW],
                                         ACT.Exp, bias=negmax[:, i:i + 1],
                                         accum_out=p_sum[:, i:i + 1]).then_inc(p_done, 1)

                def exp_zero(g):
                    tiles = slice(4 * g, 4 * g + 4)
                    act.wait_ge(z_arg_done, n * 4 + (2 * g - 2))
                    nc.scalar.activation(z_exp[:, tiles], z_arg[:, tiles], ACT.Exp).then_inc(z_exp_done, 1)

                if more:
                    spread_x(n + 1, 1 - par)
                if store:
                    take_pt(n - 1, 1)
                if attn:
                    gelu(n - 1, 1)
                if conv:
                    take_m13(n, 0)
                t_late = isinstance(n, int) and n == 1
                if more and not t_late:
                    high_t(n + 1, 1 - par)
                if store:
                    take_out(n, 0)
                    take_out(n, 1)
                if isinstance(n, int) and n == 1:
                    act.wait_ge(consts_done, 2)
                if attn:
                    for c in range(NCH):
                        act.wait_ge(q_ready, n * 2 + (c - 1))
                        nc.scalar.activation(q_sb[:, c * CH:(c + 1) * CH], work[:, 2 if c == 0 else 0, :],
                                             ACT.Identity, bias=bq_s[:, :]).then_inc(q_done, 1)
                if t_late:
                    high_t(n + 1, 1 - par)
                if conv:
                    gelu(n, 0)
                if attn:
                    for i in range(4):
                        exp(i)
                    exp_zero(0)
                if conv:
                    take_m13(n, 1)
                if attn:
                    for i in range(4, T):
                        exp(i)
                    exp_zero(1)
                if conv:
                    prime_gelu()
                    copy_x(n, par)
                if attn:
                    take_pt(n, 0)
                if is_last(n):
                    take_pt(n, 1)
                    take_out(n + 1, 0)
                    take_out(n + 1, 1)

            steady(act, body)

        @block.vector
        def _(dve):
            dve.wait_ge(filters_in, 16)
            g0, g1, g2 = (wp[:, :, :, i] for i in range(3))
            done = [0]

            def step(instruction):
                done[0] += 1
                instruction.then_inc(filters_done, 1)

            step(nc.vector.tensor_tensor(gt[:, 0, :, :], g0, g2, ALU.add))
            step(nc.vector.tensor_scalar(gt[:, 1, :, :], g2, 1 / 6, None, ALU.mult))
            step(nc.vector.tensor_scalar(gt[:, 3, :, :], g1, 1 / 12, None, ALU.mult))
            step(nc.vector.tensor_scalar(wg[:, 0, :, :], g0, 1 / 4, None, ALU.mult))
            step(nc.vector.tensor_copy(wg[:, 5, :, :], g2))
            dve.wait_ge(filters_done, 2)
            step(nc.vector.scalar_tensor_tensor(out=gt[:, 2, :, :], in0=g0, scalar=1 / 24, in1=gt[:, 1, :, :],
                                                op0=ALU.mult, op1=ALU.add))
            step(nc.vector.tensor_tensor(wg[:, 1, :, :], gt[:, 0, :, :], g1, ALU.add))
            step(nc.vector.tensor_tensor(wg[:, 2, :, :], gt[:, 0, :, :], g1, ALU.subtract))
            dve.wait_ge(filters_done, 8)
            step(nc.vector.tensor_tensor(wg[:, 3, :, :], gt[:, 2, :, :], gt[:, 3, :, :], ALU.add))
            step(nc.vector.tensor_tensor(wg[:, 4, :, :], gt[:, 2, :, :], gt[:, 3, :, :], ALU.subtract))
            step(nc.vector.tensor_scalar(wg[:, 1:3, :, :], wg[:, 1:3, :, :], -1 / 6, None, ALU.mult))
            dve.wait_ge(filters_done, 11)
            dve.wait_ge(w1t_copied, 3)

            def rows(a):
                return a.rearrange("p (r w) -> p r w", w=WIN)

            def transform_ab(n, par):
                d1, d2, d3, d4 = (xp[:, par, k, :, 1:WIN + 1] for k in range(K4))
                dve.wait_ge(x_done, n + 1)
                if from_image(n, 1):
                    dve.wait_ge(tlo_done, n * 2)
                nc.vector.scalar_tensor_tensor(out=rows(ab[:, 0, :]), in0=d2, scalar=-4.0, in1=d4, op0=ALU.mult,
                                               op1=ALU.add).then_inc(ab_done, 1)
                nc.vector.scalar_tensor_tensor(out=rows(ab[:, 1, :]), in0=d1, scalar=-4.0, in1=d3, op0=ALU.mult,
                                               op1=ALU.add).then_inc(ab_done, 1)

            def transform(n, par):
                dve.wait_ge(fcge_done, n * 3 + 3)
                f, c, g, e = fc[:, 0, :], fc[:, 1, :], ge[:, 0, :], ge[:, 1, :]
                for j, a, by, b in ((3, f, 2.0, c), (4, f, -2.0, c), (0, g, 4.0, c), (5, f, -4.0, e)):
                    nc.vector.scalar_tensor_tensor(out=t[:, T_PLACE[j], :], in0=a, scalar=by, in1=b, op0=ALU.mult,
                                                   op1=ALU.add).then_inc(td_done, 1)

            def low_weights(i):
                dve.wait_ge(whi_done, i + 1)
                nc.vector.tensor_tensor(wlo[:, M_ORDER[i], :, :], weff[i], whi[:, M_ORDER[i], :, :].bitcast(F32),
                                        ALU.subtract).then_inc(wlo_ends_done, 1)

            for dy in range(3):
                nc.vector.tensor_scalar(weff[0][:, dy, :], w1T[:, 0, :], wg[:, M_ORDER[0], 0, dy:dy + 1], None,
                                        ALU.mult).then_inc(weff_done, 1)
            for i, j in enumerate(M_ORDER):
                for m in (1, 2):
                    for dy in range(3):
                        if m == 1 and i:
                            dve.wait_ge(weff0_done, 3 * (i - 1) + dy + 1)
                        else:
                            dve.wait_ge(weff_done, 6 * i + (3 * (m - 1) if i == 0 else 3) + dy + 1)
                        nc.vector.scalar_tensor_tensor(out=weff[i][:, dy, :], in0=w1T[:, m, :],
                                                       scalar=wg[:, j, m, dy:dy + 1], in1=weff[i][:, dy, :],
                                                       op0=ALU.mult, op1=ALU.add).then_inc(weff_done, 1)
                if i == 0:
                    transform_ab(0, 0)
                    dve.wait_ge(weights_in, 16 * N_W)
                    nc.vector.tensor_copy(bq_wide[:, :], bqk[:, 0:1].to_broadcast([P, P])).then_inc(bq_wide_done, 1)
                if i == 1:
                    transform(0, 0)
                    low_weights(0)
            low_weights(NJ - 1)
            dve.wait_ge(biases_in, 48)
            dve.wait_ge(b1_ready, 1)
            nc.vector.tensor_tensor(b1eff[:, :], work[:, 2, 0:2], b1[:, :], ALU.add).then_inc(b1_done, 1)
            dve.wait_ge(small_hi_done, 2)
            nc.vector.tensor_tensor(w2lo[:, :], w2T[:, :], w2hi[:, :].bitcast(F32),
                                    ALU.subtract).then_inc(small_lo_done, 1)
            nc.vector.tensor_tensor(wqk_lo[:, :], wqk[:, :], wqk_hi[:, :].bitcast(F32),
                                    ALU.subtract).then_inc(small_lo_done, 1)
            dve.wait_ge(consts_done, 2)
            nc.vector.tensor_scalar(z_base[:, :], zeros[:, 1, :], bqk_s[:, 0:1], None,
                                    ALU.add).then_inc(z_base_done, 1)
            dve.wait_ge(z_base_done, 1)

            def combine(n, half):
                i = half + 1
                dve.wait_ge(m13_done, n * 2 + i)
                dve.wait_ge(m_ready, n * 6 + (3 * half + 2))
                if half or from_image(n, 1):
                    dve.wait_ge(y_part_done, n * 8 + 4 * half)
                nc.vector.tensor_tensor(ps_sb[:, :], m13[:, :], m_ps[:, 1, :], ALU.add).then_inc(ps_done, 1)
                nc.vector.tensor_tensor(ru_sb[:, :], m13[:, :], m_ps[:, 1, :], ALU.subtract).then_inc(ru_done, 1)

            def combine_y(n, half):
                i = half + 1
                if from_image(n, 1):
                    dve.wait_ge(hid_done, n * 2 + (half - 1))
                p, s, r, u = ps_sb[:, 0:S], ps_sb[:, S:CH], ru_sb[:, 0:S], ru_sb[:, S:CH]
                dve.wait_ge(ps_done, n * 2 + i)
                nc.vector.tensor_tensor(y[:, half, 0, :], p, s, ALU.add).then_inc(y_part_done, 1)
                nc.vector.scalar_tensor_tensor(out=y[:, half, 3, :], in0=s, scalar=4.0, in1=p, op0=ALU.mult,
                                               op1=ALU.add).then_inc(y_part_done, 1)
                dve.wait_ge(ru_done, n * 2 + i)
                nc.vector.scalar_tensor_tensor(out=y[:, half, 1, :], in0=u, scalar=8.0, in1=r, op0=ALU.mult,
                                               op1=ALU.add).then_inc(y_part_done, 1)
                nc.vector.scalar_tensor_tensor(out=y[:, half, 2, :], in0=u, scalar=2.0, in1=r, op0=ALU.mult,
                                               op1=ALU.add).then_inc(y_part_done, 1)

            def finish_y(n, half):
                dve.wait_ge(m_ready, n * 6 + (3 * half + 3))
                dve.wait_ge(y_part_done, n * 8 + (4 * half + 3))
                y03 = y[:, half, 0:2, :].rearrange("p k s -> p (k s)")
                nc.vector.tensor_tensor(y03, y03, m_ps[:, 2, :], ALU.add).then_inc(y_done, 1)

            def high_hid(n, half):
                dve.wait_ge(hid_done, n * 2 + (half + 1))
                nc.vector.tensor_copy(hid_hi[:, half, :], hid[:, half, :]).then_inc(hid_hi_done, 1)

            def take_v(n, part):
                tiles = V_PARTS[part]
                first, end = tiles[0], tiles[-1] + 1
                sums = v_bank(n, part)[:, 0:len(tiles) * VT].rearrange("p (t c) -> p t c", c=VT)
                dve.wait_ge(v_ready, n * 3 + (part - 2))
                nc.vector.tensor_tensor(v_sb[:, first:end, :], sums[:, :, 0:C],
                                        bv[:, :].unsqueeze(1).to_broadcast([P, len(tiles), C]),
                                        ALU.add).then_inc(v_done, 1)
                nc.vector.tensor_tensor(nz[:, first:end], sums[:, :, C], z_base[:, first:end],
                                        ALU.add).then_inc(v_done, 1)

            def row_max(n, j):
                pair = slice(2 * j, 2 * j + 2)
                dve.wait_ge(s_ready, n * 4 + (j - 3))
                nc.vector.tensor_reduce(negmax[:, pair],
                                        s_bank(n, j)[:, 0:2 * WINDOW].rearrange("p (a b) -> p a b", a=2), AX.X,
                                        ALU.max, negate=True).then_inc(rmax_done, 1)
                if j == 0:
                    dve.wait_ge(v_done, n * 6)
                dve.wait_ge(rmax_done, n * 4 + (j - 3))
                nc.vector.tensor_tensor(negmax[:, pair], negmax[:, pair], nz[:, pair],
                                        ALU.min).then_inc(max_done, 1)
                dve.wait_ge(max_done, n * 4 + (j - 3))
                nc.vector.tensor_tensor(z_arg[:, pair], negmax[:, pair], nz[:, pair],
                                        ALU.subtract).then_inc(z_arg_done, 1)

            def sums(n, g):
                tiles = slice(4 * g, 4 * g + 4)
                dve.wait_ge(z_exp_done, n * 2 + (g - 1))
                nc.vector.tensor_tensor(z_exp[:, tiles], z_exp[:, tiles], zeros[:, 0, tiles],
                                        ALU.mult).then_inc(sums_done, 1)
                dve.wait_ge(p_done, n * 8 + (4 * g - 4))
                dve.wait_ge(sums_done, n * 4 + (2 * g - 3))
                nc.vector.tensor_tensor(p_sum[:, tiles], p_sum[:, tiles], z_exp[:, tiles],
                                        ALU.add).then_inc(sums_done, 1)
                dve.wait_ge(sums_done, n * 4 + (2 * g - 2))
                nc.vector.reciprocal(rsum[:, tiles], p_sum[:, tiles]).then_inc(rsum_done, 1)

            def edges(n, g):
                if is_last(n) and g == 1:
                    dve.wait_ge(pn_last_done, 1)
                else:
                    dve.wait_ge(pn_done, n * 2 + (g - 1))
                first, end = 4 * g, 4 * g + 4
                a = max(first, 1)
                nc.vector.transpose(pt[P - W:P, a - 1:end - 1, P + W:WINDOW],
                                    p_sb[0:W, a:end, 0:W]).then_inc(edges_done, 1)
                e = min(end, T - 1)
                nc.vector.transpose(pt[0:W, first + 1:e + 1, 0:W],
                                    p_sb[P - W:P, first:e, P + W:WINDOW]).then_inc(edges_done, 1)

            def add_h(n, g):
                cols = slice(g * CH, (g + 1) * CH)
                dve.wait_ge(o_ready, n * 2 + (g - 3))
                nc.vector.tensor_tensor(o_sb[:, cols], work[:, g, :], h[:, cols], ALU.add).then_inc(o_done, 1)

            def low_hid_last(n):
                dve.wait_ge(hid_hi_done, n * 2 + 2)
                for c in range(NCH):
                    cols = slice(c * CH, (c + 1) * CH)
                    nc.vector.tensor_tensor(hid_lo[:, 1, cols], hid[:, 1, cols], hid_hi[:, 1, cols].bitcast(F32),
                                            ALU.subtract).then_inc(hid_lo_last_done, 1)

            def normalise_last(n):
                tiles = slice(T // 2, T)
                dve.wait_ge(rsum_done, n * 2)
                nc.vector.tensor_tensor(p_sb[:, tiles, :], p_sb[:, tiles, :],
                                        rsum[:, tiles].unsqueeze(2).to_broadcast([P, T // 2, WINDOW]),
                                        ALU.mult).then_inc(pn_last_done, 1)

            def sum_h(n):
                by_plane = h.rearrange("p (s k) -> p k s", k=K4)
                if is_last(n):
                    dve.wait_ge(o_done, n * 2 - 2)
                for i, step in enumerate((3, 1)):
                    k = PLANES[2 * i]
                    dve.wait_ge(up_ready, n * 2 + (i - 1))
                    dve.wait_ge(xr_done, n * 2)
                    nc.vector.scalar_tensor_tensor(
                        out=by_plane[:, k:k + step + 1:step, :],
                        in0=up_bank(n, i).rearrange("p (k s) -> p k s", k=2), scalar=b2[:, 0:1],
                        in1=xr[:, 2 * i:2 * i + 2, :], op0=ALU.add, op1=ALU.add).then_inc(h_done, 1)
                dve.wait_ge(h_done, n * 2)
                for c in range(NCH):
                    cols = slice(c * CH, (c + 1) * CH)
                    nc.vector.tensor_copy(h_hi[:, cols], h[:, cols]).then_inc(h_hi_done, 1)
                for c in range(NCH):
                    cols = slice(c * CH, (c + 1) * CH)
                    dve.wait_ge(h_hi_done, n * 2 + (c - 1))
                    nc.vector.tensor_tensor(h_lo[:, cols], h[:, cols], h_hi[:, cols].bitcast(F32),
                                            ALU.subtract).then_inc(h_lo_done, 1)

            def body(n, par, conv, attn, store, more):
                if isinstance(n, int) and n == 0:
                    combine(n, 0)
                if more:
                    transform_ab(n + 1, 1 - par)
                if attn:
                    high_hid(n - 1, 1)
                if is_last(n):
                    low_hid_last(n - 1)
                if store:
                    add_h(n, 0)
                if isinstance(n, int) and n == 1:
                    combine(n, 0)
                    sum_h(n)
                if more:
                    transform(n + 1, 1 - par)
                if store:
                    add_h(n, 1)
                if from_image(n, 2):
                    if conv:
                        combine(n, 0)
                    if attn:
                        sum_h(n)
                if conv:
                    combine_y(n, 0)
                    finish_y(n, 0)
                if attn:
                    for part in range(len(V_PARTS)):
                        take_v(n, part)
                if attn:
                    row_max(n, 0)
                    row_max(n, 1)
                if conv:
                    high_hid(n, 0)
                if attn:
                    row_max(n, 2)
                    sums(n, 0)
                    row_max(n, 3)
                if is_last(n):
                    edges(n, 0)
                    sums(n, 1)
                    normalise_last(n)
                    edges(n, 1)
                    add_h(n + 1, 0)
                    add_h(n + 1, 1)
                    return
                if attn:
                    sums(n, 1)
                    edges(n, 0)
                if conv:
                    combine(n, 1)
                    combine_y(n, 1)
                if conv:
                    finish_y(n, 1)
                if attn:
                    edges(n, 1)

            steady(dve, body)

        @block.gpsimd
        def _(pool):
            nc.gpsimd.memset(xp[:, :, :, :, :], 0.0).then_inc(zeroed, 1)
            nc.gpsimd.memset(h_around[:, 0:W], 0.0).then_inc(zeroed, 1)
            nc.gpsimd.memset(h_around[:, W + PIX:], 0.0).then_inc(zeroed, 1)
            nc.gpsimd.memset(pt[:, :, :], 0.0).then_inc(zeroed, 1)

            def differences(n, par):
                def plane(k, shift=0):
                    return xp[:, par, k, :, 1 + shift:WIN + 1 + shift]

                def rows(a):
                    return a.rearrange("p (r w) -> p r w", w=WIN)

                pool.wait_ge(x_done, n + 1)
                if from_image(n, 1):
                    pool.wait_ge(td_done, n * 4)
                nc.gpsimd.tensor_tensor(fc[:, :, :].rearrange("p a (r w) -> p a r w", w=WIN),
                                        xp[:, par, 2:4, :, 1:WIN + 1], xp[:, par, 0:2, :, 1:WIN + 1],
                                        ALU.subtract).then_inc(fcge_done, 1)
                nc.gpsimd.tensor_tensor(rows(ge[:, 0, :]), plane(3, -1), plane(1), ALU.subtract).then_inc(fcge_done, 1)
                nc.gpsimd.tensor_tensor(rows(ge[:, 1, :]), plane(0, 1), plane(2), ALU.subtract).then_inc(fcge_done, 1)
                pool.wait_ge(ab_done, n * 2 + 2)
                nc.gpsimd.tensor_tensor(t[:, T_PLACE[1], :], ab[:, 0, :], ab[:, 1, :], ALU.add).then_inc(tp_done, 1)
                nc.gpsimd.tensor_tensor(t[:, T_PLACE[2], :], ab[:, 0, :], ab[:, 1, :],
                                        ALU.subtract).then_inc(tp_done, 1)

            def low_t(n, par, i):
                part = T_PARTS[i]
                pool.wait_ge(thi_done, n * 2 + (i + 1))
                nc.gpsimd.tensor_tensor(tlo[:, par, part, :], t[:, part, :], thi[:, par, part, :].bitcast(F32),
                                        ALU.subtract).then_inc(tlo_done, 1)

            def low_hid(n, half, c):
                cols = slice(c * CH, (c + 1) * CH)
                pool.wait_ge(hid_hi_done, n * 2 + (half + 1))
                nc.gpsimd.tensor_tensor(hid_lo[:, half, cols], hid[:, half, cols],
                                        hid_hi[:, half, cols].bitcast(F32), ALU.subtract).then_inc(hid_lo_done, 1)

            def normalise(n, g):
                tiles = slice(4 * g, 4 * g + 4)
                pool.wait_ge(rsum_done, n * 2 + (g - 1))
                nc.gpsimd.tensor_tensor(p_sb[:, tiles, :], p_sb[:, tiles, :],
                                        rsum[:, tiles].unsqueeze(2).to_broadcast([P, 4, WINDOW]),
                                        ALU.mult).then_inc(pn_done, 1)

            differences(0, 0)
            low_t(0, 0, 0)
            for i in range(1, NJ - 1):
                j = M_ORDER[i]
                pool.wait_ge(whi_done, i + 1)
                nc.gpsimd.tensor_tensor(wlo[:, j, :, :], weff[i], whi[:, j, :, :].bitcast(F32),
                                        ALU.subtract).then_inc(wlo_done, 1)
                if i == 2:
                    low_t(0, 0, 1)

            def body(n, par, conv, attn, store, more):
                hidden_first = isinstance(n, int) and n == 1
                if hidden_first:
                    for c in range(NCH):
                        low_hid(n - 1, 1, c)
                if more:
                    differences(n + 1, 1 - par)
                if attn and not hidden_first and not is_last(n):
                    for c in range(NCH):
                        low_hid(n - 1, 1, c)
                if more:
                    for i in range(len(T_PARTS)):
                        low_t(n + 1, 1 - par, i)
                for c in range(NCH):
                    if conv:
                        low_hid(n, 0, c)
                    if attn and not (is_last(n) and c == 1):
                        normalise(n, c)

            steady(pool, body)


_INS = ["x", "L0_conv_w_perc", "L0_conv_b_perc", "L0_conv_w_up1", "L0_conv_b_up1", "L0_conv_w_up2",
        "L0_conv_b_up2", "L0_conv_w_qkv", "L0_conv_b_qkv"]


def kernel(**inputs):
    import concourse.bacc as bacc
    import ml_dtypes
    from concourse.bass_utils import run_bass_kernel_spmd as run

    nc = bacc.Bacc("TRN2", target_bir_lowering=False, num_devices=1)
    arrays = {name: np.ascontiguousarray(inputs[name]) for name in _INS}
    arrays["identity"] = np.eye(P, dtype=np.float32)
    arrays["identity_bf16"] = np.eye(P, dtype=ml_dtypes.bfloat16)
    arrays["masks"] = window_masks(ml_dtypes.bfloat16)
    arrays["zero_keys"] = zero_keys()
    args = [nc.dram_tensor(name, a.shape, mybir.dt.from_np(a.dtype), kind="ExternalInput").ap()
            for name, a in arrays.items()]
    out = nc.dram_tensor("out", (B, H, W, C), F32, kind="ExternalOutput").ap()
    build(nc, *args, out)
    r = run(nc, [arrays], core_ids=[0])
    return r.results[0]["out"]
```
